# Optimizing a Trainium2 kernel written in Bass

```python
import numpy as np
import jax
import jax.numpy as jnp

def _softmax(x, axis=-1):
    return jax.nn.softmax(x, axis=axis)

def _gelu(x):
    return jax.nn.gelu(x, approximate=True)

def _silu(x):
    return jax.nn.silu(x)

def _sigmoid(x):
    return jax.nn.sigmoid(x)

def _layernorm(x, axis=-1, eps=1e-05):
    m = jnp.mean(x, axis=axis, keepdims=True)
    v = jnp.var(x, axis=axis, keepdims=True)
    return (x - m) / jnp.sqrt(v + eps)

def _scatter_add(tgt, idx, src, axis=0):
    return tgt.at[idx].add(src)

def _segment_sum(src, seg, n):
    return jax.ops.segment_sum(src, seg, n)
kernel_name = 'mk_adj_preln_d4_adj_r2_bcae93'

def setup_inputs(seed: int=0):
    np.random.seed(seed)
    _w = jnp.asarray

    def _rec_inputs():
        import jax
        import jax.numpy as jnp
        _gk = jax.random.key(seed)
        x = -0.0002928 + 1 * jax.random.normal(jax.random.fold_in(_gk, 1), (128, 128, 256), jnp.float32)
        _a = jax.random.bernoulli(jax.random.fold_in(_gk, 2), 0.03125, (128, 128, 128))
        _a = jnp.logical_or(_a, jnp.swapaxes(_a, -1, -2))
        _a = jnp.logical_or(_a, jnp.eye(128, dtype=bool))
        _af = _a.astype(jnp.float32)
        _af = _af * jax.random.uniform(jax.random.fold_in(_gk, 3), (128, 128, 128), jnp.float32, 0.05, 1)
        adj = _af
        return (x, adj)
    x, adj = _rec_inputs()

    def _L0_gnn_setup():
        import jax, jax.numpy as jnp
        import numpy as np
        B, N, DIN, DOUT, K = (4, 1024, 256, 256, 3)
        key = jax.random.key(seed)
        ks = jax.random.split(key, 8)
        X = jax.random.normal(ks[0], (B, N, DIN), dtype=jnp.float32)
        A = jax.random.uniform(ks[1], (B, N, N), dtype=jnp.float32)
        Wv = jax.random.normal(ks[2], (DIN, DOUT), dtype=jnp.float32) * 0.02
        bv = jax.random.normal(ks[3], (DOUT,), dtype=jnp.float32) * 0.02
        aw = jax.random.normal(ks[4], (2 * DOUT, 1), dtype=jnp.float32) * 0.05
        ab = jax.random.normal(ks[5], (1,), dtype=jnp.float32) * 0.05
        Wk = jax.random.normal(ks[6], (K, DIN, DOUT), dtype=jnp.float32) * 0.02
        bk = jax.random.normal(ks[7], (K, DOUT), dtype=jnp.float32) * 0.02
        return {'X': X, 'A': A, 'Wv': Wv, 'bv': bv, 'aw': aw, 'ab': ab, 'Wk': Wk, 'bk': bk}
    _L0_gnn_all = _L0_gnn_setup()
    _L0_gnn_in = {k: v for k, v in _L0_gnn_all.items() if k in ('Wv', 'bv', 'aw', 'ab', 'Wk', 'bk')}
    del _L0_gnn_all

    def _L1_gnn_setup():
        import jax, jax.numpy as jnp
        import numpy as np
        EPS_LN = 1e-05

        def hypergraph_conv(x, adj, W, b):
            N, C, _ = adj.shape
            H = (adj != 0).astype(x.dtype)
            w = adj.reshape(N, -1)[:, :C]
            xw = jnp.einsum('ncd,hd->nch', x, W)
            Dn = jnp.einsum('nce,ne->nc', H, w)
            Dn = jnp.where(Dn > 0, 1.0 / Dn, 0.0)
            Be = H.sum(axis=1)
            Be = jnp.where(Be > 0, 1.0 / Be, 0.0)
            m = Be[:, :, None] * jnp.einsum('nce,nch->neh', H, xw)
            out = Dn[:, :, None] * jnp.einsum('nce,neh->nch', H, m)
            return out + b

        def layer_norm(x, g, b):
            mu = jnp.mean(x, axis=-1, keepdims=True)
            var = jnp.var(x, axis=-1, keepdims=True)
            return (x - mu) * jax.lax.rsqrt(var + EPS_LN) * g + b
        key = jax.random.key(seed)
        ks = jax.random.split(key, 4)
        N, C, Din, Dh, Dout = (16, 512, 256, 512, 256)
        x = jax.random.normal(ks[0], (N, C, Din), dtype=jnp.float32)
        adj = jax.random.uniform(ks[1], (N, C, C), dtype=jnp.float32, minval=0.1, maxval=1.0)
        W1 = jax.random.normal(ks[2], (Dh, Din), dtype=jnp.float32) * (1.0 / np.sqrt(Din))
        b1 = jnp.zeros((Dh,), dtype=jnp.float32)
        gamma = jnp.ones((Dh,), dtype=jnp.float32)
        beta = jnp.zeros((Dh,), dtype=jnp.float32)
        W2 = jax.random.normal(ks[3], (Dout, Dh), dtype=jnp.float32) * (1.0 / np.sqrt(Dh))
        b2 = jnp.zeros((Dout,), dtype=jnp.float32)
        return {'x': x, 'adj': adj, 'W1': W1, 'b1': b1, 'gamma': gamma, 'beta': beta, 'W2': W2, 'b2': b2}
    _L1_gnn_all = _L1_gnn_setup()
    _L1_gnn_in = {k: v for k, v in _L1_gnn_all.items() if k in ('W1', 'b1', 'gamma', 'beta', 'W2', 'b2')}
    del _L1_gnn_all

    def _L2_gnn_setup():
        import jax, jax.numpy as jnp
        import numpy as np
        IN_DIM = 256
        ATT_DIM = 64
        B, N = (4, 2048)
        key = jax.random.key(seed)
        k1, k2, k3, k4 = jax.random.split(key, 4)
        x = jax.random.normal(k1, (B, N, IN_DIM), dtype=jnp.float32)
        adj_matrix = (jax.random.uniform(k2, (B, N, N)) < 0.05).astype(jnp.float32)
        W_qk = jax.random.normal(k3, (2 * ATT_DIM, IN_DIM), dtype=jnp.float32) / np.sqrt(IN_DIM)
        W_v = jax.random.normal(k4, (IN_DIM, IN_DIM), dtype=jnp.float32) / np.sqrt(IN_DIM)
        return {'x': x, 'adj_matrix': adj_matrix, 'W_qk': W_qk, 'W_v': W_v}
    _L2_gnn_all = _L2_gnn_setup()
    _L2_gnn_in = {k: v for k, v in _L2_gnn_all.items() if k in ('W_qk', 'W_v')}
    del _L2_gnn_all

    def _L3_gnn_setup():
        import jax, jax.numpy as jnp
        import numpy as np
        EPS = 1e-06
        key = jax.random.key(seed)
        k1, k2, k3 = jax.random.split(key, 3)
        B, N, F, O = (8, 2048, 256, 256)
        x = jax.random.normal(k1, (B, N, F), dtype=jnp.float32)
        adj = jax.random.uniform(k2, (B, N, N), dtype=jnp.float32)
        W = jax.random.normal(k3, (O, 2 * F), dtype=jnp.float32) * (1.0 / np.sqrt(2 * F))
        return {'x': x, 'adj': adj, 'W': W}
    _L3_gnn_all = _L3_gnn_setup()
    _L3_gnn_in = {k: v for k, v in _L3_gnn_all.items() if k in ('W',)}
    del _L3_gnn_all
    return {'x': x, 'adj': adj, 'L0_gnn_Wv': _L0_gnn_in['Wv'], 'L0_gnn_bv': _L0_gnn_in['bv'], 'L0_gnn_aw': _L0_gnn_in['aw'], 'L0_gnn_ab': _L0_gnn_in['ab'], 'L0_gnn_Wk': _L0_gnn_in['Wk'], 'L0_gnn_bk': _L0_gnn_in['bk'], 'L1_gnn_W1': _L1_gnn_in['W1'], 'L1_gnn_b1': _L1_gnn_in['b1'], 'L1_gnn_gamma': _L1_gnn_in['gamma'], 'L1_gnn_beta': _L1_gnn_in['beta'], 'L1_gnn_W2': _L1_gnn_in['W2'], 'L1_gnn_b2': _L1_gnn_in['b2'], 'L2_gnn_W_qk': _L2_gnn_in['W_qk'], 'L2_gnn_W_v': _L2_gnn_in['W_v'], 'L3_gnn_W': _L3_gnn_in['W']}

def reference(x, adj, L0_gnn_Wv, L0_gnn_bv, L0_gnn_aw, L0_gnn_ab, L0_gnn_Wk, L0_gnn_bk, L1_gnn_W1, L1_gnn_b1, L1_gnn_gamma, L1_gnn_beta, L1_gnn_W2, L1_gnn_b2, L2_gnn_W_qk, L2_gnn_W_v, L3_gnn_W):
    import jax
    import jax.numpy as jnp

    def _L0_gnn_ref(X, A, Wv, bv, aw, ab, Wk, bk):
        import jax, jax.numpy as jnp
        import numpy as np
        B, N, DIN, DOUT, K = (4, 1024, 256, 256, 3)
        d = Wv.shape[1]
        Xw = X @ Wv + bv
        sj = Xw @ aw[:d, 0]
        si = Xw @ aw[d:, 0]
        e = jax.nn.leaky_relu(sj[:, None, :] + si[:, :, None] + ab[0], negative_slope=0.2)
        alpha_matrix = A * jnp.exp(e)
        transition = alpha_matrix / (jnp.sum(alpha_matrix, axis=-1, keepdims=True) + 1e-12)
        H = jnp.zeros(X.shape[:-1] + (d,), dtype=X.dtype)
        Xk = X
        for k in range(Wk.shape[0]):
            H = H + Xk @ Wk[k] + bk[k]
            Xk = jnp.einsum('bij,bjd->bid', transition, Xk)
        return jax.nn.relu(H)

    def _L1_gnn_ref(x, adj, W1, b1, gamma, beta, W2, b2):
        import jax, jax.numpy as jnp
        import numpy as np
        EPS_LN = 1e-05

        def hypergraph_conv(x, adj, W, b):
            N, C, _ = adj.shape
            H = (adj != 0).astype(x.dtype)
            w = adj.reshape(N, -1)[:, :C]
            xw = jnp.einsum('ncd,hd->nch', x, W)
            Dn = jnp.einsum('nce,ne->nc', H, w)
            Dn = jnp.where(Dn > 0, 1.0 / Dn, 0.0)
            Be = H.sum(axis=1)
            Be = jnp.where(Be > 0, 1.0 / Be, 0.0)
            m = Be[:, :, None] * jnp.einsum('nce,nch->neh', H, xw)
            out = Dn[:, :, None] * jnp.einsum('nce,neh->nch', H, m)
            return out + b

        def layer_norm(x, g, b):
            mu = jnp.mean(x, axis=-1, keepdims=True)
            var = jnp.var(x, axis=-1, keepdims=True)
            return (x - mu) * jax.lax.rsqrt(var + EPS_LN) * g + b
        h = jax.nn.relu(hypergraph_conv(x, adj, W1, b1))
        h = layer_norm(h, gamma, beta)
        y = hypergraph_conv(h, adj, W2, b2)
        return y + x

    def _L2_gnn_ref(x, adj_matrix, W_qk, W_v):
        import jax, jax.numpy as jnp
        import numpy as np
        IN_DIM = 256
        ATT_DIM = 64
        B, N = (4, 2048)
        qk = jnp.einsum('bnd,ed->bne', x, W_qk)
        q, k = jnp.split(qk, 2, axis=-1)
        v = jnp.einsum('bnd,ed->bne', x, W_v)
        inv_scale = 1.0 / ATT_DIM ** 0.5
        scores = jnp.einsum('bnd,bmd->bnm', q, k) * inv_scale
        w = jnp.sum(scores * adj_matrix, axis=-1, keepdims=True)
        w = jax.nn.softmax(w, axis=1)
        return w * v

    def _L3_gnn_ref(x, adj, W):
        import jax, jax.numpy as jnp
        import numpy as np
        EPS = 1e-06
        deg = jnp.sum(adj, axis=-1, keepdims=True)
        agg = jnp.einsum('bij,bjf->bif', adj, x) / jnp.maximum(deg, EPS)
        cat = jnp.concatenate([x, agg], axis=2)
        out = jnp.einsum('bnf,of->bno', cat, W)
        return jax.nn.relu(out)
    h = jnp.maximum(_layernorm(x, axis=-1), 0.0)
    x = x + _L0_gnn_ref(h, adj, L0_gnn_Wv, L0_gnn_bv, L0_gnn_aw, L0_gnn_ab, L0_gnn_Wk, L0_gnn_bk)
    h = jnp.maximum(_layernorm(x, axis=-1), 0.0)
    x = x + _L1_gnn_ref(h, adj, L1_gnn_W1, L1_gnn_b1, L1_gnn_gamma, L1_gnn_beta, L1_gnn_W2, L1_gnn_b2)
    h = jnp.maximum(_layernorm(x, axis=-1), 0.0)
    x = x + _L2_gnn_ref(h, adj, L2_gnn_W_qk, L2_gnn_W_v)
    h = jnp.maximum(_layernorm(x, axis=-1), 0.0)
    x = x + _L3_gnn_ref(h, adj, L3_gnn_W)
    return x

_drawn_inputs = setup_inputs


def setup_inputs(seed=0):
    import zlib

    import numpy as np

    out = dict(_drawn_inputs(seed))
    spreads = {'L1_gnn_b1': (0.0, 0.1),
     'L1_gnn_gamma': (1.0, 0.2),
     'L1_gnn_beta': (0.0, 0.1),
     'L1_gnn_b2': (0.0, 0.8)}
    factors = {'L0_gnn_Wv': 8.0,
     'L0_gnn_bv': 184.167,
     'L0_gnn_aw': 8.0,
     'L2_gnn_W_qk': 8.0,
     'L2_gnn_W_v': 8.0}
    for name, (base, spread) in spreads.items():
        noise = np.random.default_rng([zlib.crc32(name.encode()), seed]).standard_normal(out[name].shape)
        drawn = base * np.exp(spread * noise) if base else spread * noise
        out[name] = jnp.asarray(drawn.astype(out[name].dtype))
    for name, factor in factors.items():
        out[name] = (out[name] * factor).astype(out[name].dtype)
    return out
```

```python
from contextlib import ExitStack

import concourse.bass as bass
from concourse import mybir

F32 = mybir.dt.float32
F32R = mybir.dt.float32r
ALU = mybir.AluOpType
ACT = mybir.ActivationFunctionType
AX_X = mybir.AxisListType.X

LN_EPS = 1e-5
ROW_EPS = 1e-12
DEG_EPS = 1e-6
SLOPE = 0.2
TINY = 1e-38
UNROLL = 4


def build_program(nc, x, adj, l0_wv, l0_bv, l0_aw, l0_ab, l0_wk, l0_bk, l1_w1, l1_b1, l1_gamma,
                  l1_beta, l1_w2, l1_b2, l2_wqk, l2_wv, l3_w, out):
    graphs, N, D = x.shape
    G = 2
    PAIRS = graphs // G
    KD = D // N
    HID = l1_w1.shape[0]
    KH = HID // N
    ATT = l2_wqk.shape[0] // 2
    HOPS = l0_wk.shape[0]
    assert N == 128 and D == 256 and HID == 512 and HOPS == 3 and ATT == 64 and PAIRS % UNROLL == 0

    x_pairs = x.rearrange("(p g) n d -> p n g d", g=G)
    adj_pairs = adj.rearrange("(p g) i j -> p i g j", g=G)
    out_pairs = out.rearrange("(p g) n d -> p n g d", g=G)

    with ExitStack() as ctx:
        def sb(name, shape, dt=F32):
            return ctx.enter_context(nc.sbuf_tensor(name, shape, dt))

        def sem(name):
            return ctx.enter_context(nc.semaphore(name))

        def split(name, shape):
            return sb(name + "_hi", shape, F32R), sb(name + "_lo", shape, F32R)

        ident = sb("ident", [N, N])
        ones_r = sb("ones_r", [N, N], F32R)
        eps_ln = sb("eps_ln", [N, G])
        minus_half = sb("minus_half", [N, G])
        u_hi, u_lo = split("u", [N, KD, 2])
        s_const = sb("s_const", [N, 1])
        wk_hi, wk_lo = split("wk", [N, KD, HOPS, D])
        w1_hi, w1_lo = split("w1", [N, KD, HID])
        w2_hi, w2_lo = split("w2", [N, KH, D])
        bw_hi, bw_lo = split("bw", [N, D])
        wqk_hi, wqk_lo = split("wqk", [N, KD, 2 * ATT])
        wv_hi, wv_lo = split("wv", [N, KD, D])
        w3_hi, w3_lo = split("w3", [N, 2 * KD, D])
        BK, B1, B2 = slice(0, D), slice(D, D + HID), slice(D + HID, 2 * D + HID)
        bias_f = sb("bias_f", [N, 2 * D + HID])
        bias_r = sb("bias_r", [N, 2 * D + HID], F32R)

        n_wv0 = sb("n_wv0", [N, KD, D])
        n_wk = sb("n_wk", [N, KD, HOPS, D])
        n_w1 = sb("n_w1", [N, KH, D])
        n_w2 = sb("n_w2", [N, KD, HID])
        n_wqk = sb("n_wqk", [N, D])
        n_wv2 = sb("n_wv2", [N, KD, D])
        n_w3 = sb("n_w3", [N, KD, 2 * D])
        aw_rows = sb("aw_rows", [N, 2, D])
        bv_rows = sb("bv_rows", [N, D])
        ab_rows = sb("ab_rows", [N, 1])
        gamma_t = sb("gamma_t", [N, KH])
        beta_t = sb("beta_t", [N, KH])
        u_f = sb("u_f", [N, KD, 2])
        kappa = sb("kappa", [N, 2])
        kappa1 = sb("kappa1", [N, 1])
        junk = sb("junk", [N, D])
        t_wqk = sb("t_wqk", [N, KD, 2 * ATT])

        x_in = sb("x_in", [N, UNROLL, G, D])
        a_in = sb("a_in", [N, UNROLL, G, N])
        deg = sb("deg", [N, G])
        deg_max = sb("deg_max", [N, G])
        deg_inv = sb("deg_inv", [N, G])
        w_scale = sb("w_scale", [N, UNROLL, G])
        a_mean = sb("a_mean", [N, G, N])
        amT_hi, amT_lo = split("amT", [N, UNROLL, G, N])
        inc_t = sb("inc_t", [N, G, N])
        edge_w = sb("edge_w", [N, G])
        edge_cnt = sb("edge_cnt", [N, G])
        edge_cnt1 = sb("edge_cnt1", [N, G])
        edge_inv = sb("edge_inv", [N, G])
        binc_t = sb("binc_t", [N, G, N])
        node_w1 = sb("node_w1", [N, G])
        node_w2 = sb("node_w2", [N, G])
        node_inv = sb("node_inv", [N, G])
        prop = sb("prop", [N, G, N])
        ptT_hi, ptT_lo = split("ptT", [N, 2, 2, G, N])
        pT_hi, pT_lo, tT_hi, tT_lo = ptT_hi[:, :, 0], ptT_lo[:, :, 0], ptT_hi[:, :, 1], ptT_lo[:, :, 1]
        stats = [sb(f"stats{n}", [N, G, 6]) for n in range(5)]
        moments = [sb(f"moments{n}", [N, G, 2]) for n in range(5)]
        var_eps = [sb(f"var_eps{n}", [N, G]) for n in range(5)]
        rstd = [sb(f"rstd{n}", [N, G]) for n in range(5)]
        normed = [sb(f"normed{n}", [N, G, D]) for n in range(4)]
        held = sb("held", [N, 1])

        h0T_hi, h0T_lo = split("h0T", [N, G * KD, N])
        s_sb = sb("s_sb", [N, G, 2])
        y2_hi, y2_lo = split("y2", [N, G, D])
        y1_hi, y1_lo = split("y1", [N, G, D])
        z = sb("z", [N, G, N])
        z_leaky = sb("z_leaky", [N, G, N])
        z_exp = sb("z_exp", [N, G, N])
        alpha = sb("alpha", [N, G, N])
        row_sum = sb("row_sum", [N, G])
        row_sum1 = sb("row_sum1", [N, G])
        row_inv = sb("row_inv", [N, G])
        trans = sb("trans", [N, G, N])
        x1 = sb("x1", [N, G, D])

        h1 = sb("h1", [N, G, D])
        h1_hi, h1_lo = split("h1", [N, G, D])
        xh = sb("xh", [N, 2, G, D])
        ph_hi, ph_lo = split("ph", [N, G * KD, N])
        r = sb("r", [N, G, HID])
        rc = sb("rc", [N, G, HID])
        rc_hi, rc_lo = split("rc", [N, G, HID])
        pr_hi, pr_lo = split("pr", [N, G, KH, N])
        x2 = sb("x2", [N, 2, G, D])

        h2T_hi, h2T_lo = split("h2T", [N, G * KD, N])
        q_sb = sb("q_sb", [N, G, ATT])
        k_hi, k_lo = split("k", [N, G, ATT])
        qk_junk = sb("qk_junk", [N, G, ATT])
        w = sb("w", [N, G])
        w_nmax = sb("w_nmax", [N, G])
        w_junk = sb("w_junk", [N, G, N])
        w_sum = sb("w_sum", [N, G])
        w_exp = sb("w_exp", [N, G])
        w_inv = sb("w_inv", [N, G])
        w_soft = sb("w_soft", [N, G])
        x3 = sb("x3", [N, G, D])

        h3T_hi, h3T_lo = split("h3T", [N, G * KD, N])
        zb_hi, zb_lo = split("zb", [N, G, D])
        x4 = sb("x4", [N, G, D])

        t_w1 = r
        t_w2 = rc[:].rearrange("p g (c d) -> p (g c) d", d=D)
        t_w2g = xh[:].rearrange("p s g d -> p (s g) d")
        t_w3 = x2[:].rearrange("p s g d -> p (s g) d")
        t_wv = x3

        bank = [ctx.enter_context(nc.psum_tensor(f"bank{b}", [N, 512], F32)) for b in range(8)]

        def halves(b, first=0):
            return bank[b][:, first:first + G * N].rearrange("p (g n) -> p g n", g=G)

        def wide(b):
            return bank[b][:, :].rearrange("p (g d) -> p g d", g=G)

        h0T_ps, y1_ps = bank[0], wide(0)
        y2_ps, y0_ps = wide(1), wide(1)
        e_ps, pT_ps, wrow_ps = halves(2), halves(2), halves(2)
        s_ps = bank[2][:, 256:260].rearrange("p (g s) -> p g s", g=G)
        tT_ps = halves(2, 256)
        ph_ps = bank[3]
        r_ps = [bank[4], bank[3]]
        pr_ps = [bank[4], bank[3]]
        conv_ps = wide(4)
        v_ps, h3T_ps, out_ps = wide(5), bank[5], wide(5)
        aT_ps, amT_ps = halves(6), halves(6, 256)
        gram_ps = halves(6)
        node_ps = bank[6][:, 256:256 + G]
        h2T_ps = bank[6]
        qk_ps = halves(6)
        ak_ps = bank[6][:, 256:256 + G * ATT].rearrange("p (g a) -> p g a", g=G)
        zb_ps = wide(7)

        zeroed = sem("zeroed")
        consts = sem("consts")
        loaded = sem("loaded")
        bias_in = sem("bias_in")
        turned = sem("turned")
        turned_sb = sem("turned_sb")
        w2_scaled = sem("w2_scaled")
        bw_ready = sem("bw_ready")
        u_ready = sem("u_ready")
        kappa_ready = sem("kappa_ready")
        hi_ready = sem("hi_ready")
        weights_ready = sem("weights_ready")

        pair_loaded = [sem(f"pair_loaded{k}") for k in range(UNROLL)]
        stored = sem("stored")
        stats_done = [sem(f"stats_done{n}") for n in range(4)]
        moments_done = [sem(f"moments_done{n}") for n in range(4)]
        var_done = [sem(f"var_done{n}") for n in range(4)]
        rstd_done = [sem(f"rstd_done{n}") for n in range(4)]
        normed_done = [sem(f"normed_done{n}") for n in range(4)]
        r_stats_done = [sem(f"r_stats_done{g}") for g in range(G)]
        r_moments_done = [sem(f"r_moments_done{g}") for g in range(G)]
        r_var_done = [sem(f"r_var_done{g}") for g in range(G)]
        r_rstd_done = [sem(f"r_rstd_done{g}") for g in range(G)]
        deg_done = sem("deg_done")
        deg_max_done = sem("deg_max_done")
        deg_inv_done = sem("deg_inv_done")
        a_mean_done = sem("a_mean_done")
        aT_ready = sem("aT_ready")
        amT_hi_done = sem("amT_hi_done")
        amT_done = sem("amT_done")
        inc_done = sem("inc_done")
        edge_cnt_done = sem("edge_cnt_done")
        edge_cnt1_done = sem("edge_cnt1_done")
        edge_inv_done = sem("edge_inv_done")
        binc_done = sem("binc_done")
        gram_ready = sem("gram_ready")
        node_w1_done = sem("node_w1_done")
        node_w2_done = sem("node_w2_done")
        node_inv_done = sem("node_inv_done")
        prop_done = sem("prop_done")

        h0T_ready = sem("h0T_ready")
        h0T_hi_done = sem("h0T_hi_done")
        h0T_done = sem("h0T_done")
        s_ready = sem("s_ready")
        s_done = sem("s_done")
        y2_ready = sem("y2_ready")
        y2_hi_done = sem("y2_hi_done")
        y2_done = sem("y2_done")
        e_ready = sem("e_ready")
        z_done = sem("z_done")
        leaky_done = sem("leaky_done")
        exp_done = sem("exp_done")
        alpha_done = sem("alpha_done")
        row_sum_done = sem("row_sum_done")
        row_inv_done = sem("row_inv_done")
        trans_done = sem("trans_done")
        ptT_ready = sem("ptT_ready")
        ptT_hi_done = sem("ptT_hi_done")
        ptT_done = sem("ptT_done")
        y1_ready = sem("y1_ready")
        y1_hi_done = sem("y1_hi_done")
        y1_done = sem("y1_done")
        y0_ready = sem("y0_ready")
        x1_done = sem("x1_done")

        h1_done = sem("h1_done")
        h1_hi_done = sem("h1_hi_done")
        h1_lo_done = sem("h1_lo_done")
        xh_done = sem("xh_done")
        ph_ready = sem("ph_ready")
        ph_hi_done = sem("ph_hi_done")
        ph_done = sem("ph_done")
        r_ready = [sem(f"r_ready{g}") for g in range(G)]
        r_done = [sem(f"r_done{g}") for g in range(G)]
        rc_done = [sem(f"rc_done{g}") for g in range(G)]
        rc_hi_done = [sem(f"rc_hi_done{g}") for g in range(G)]
        rc_lo_done = [sem(f"rc_lo_done{g}") for g in range(G)]
        pr_ready = [sem(f"pr_ready{g}") for g in range(G)]
        pr_hi_done = [sem(f"pr_hi_done{g}") for g in range(G)]
        pr_done = [sem(f"pr_done{g}") for g in range(G)]
        conv_ready = sem("conv_ready")
        x2_done = sem("x2_done")

        h2T_ready = sem("h2T_ready")
        h2T_hi_done = sem("h2T_hi_done")
        h2T_done = sem("h2T_done")
        qk_ready = sem("qk_ready")
        q_done = sem("q_done")
        k_done = sem("k_done")
        ak_ready = sem("ak_ready")
        w_done = sem("w_done")
        wrow_ready = sem("wrow_ready")
        w_nmax_done = sem("w_nmax_done")
        w_exp_done = sem("w_exp_done")
        w_inv_done = sem("w_inv_done")
        w_soft_done = sem("w_soft_done")
        v_ready = sem("v_ready")
        x3_done = sem("x3_done")

        h3T_ready = sem("h3T_ready")
        h3T_hi_done = sem("h3T_hi_done")
        h3T_done = sem("h3T_done")
        zb_ready = sem("zb_ready")
        zb_hi_done = sem("zb_hi_done")
        zb_done = sem("zb_done")
        out_ready = sem("out_ready")
        x4_done = sem("x4_done")

        SPLITS = [(n_wk[:], wk_hi[:], wk_lo[:]), (t_w1[:], w1_hi[:], w1_lo[:]),
                  (t_wqk[:], wqk_hi[:], wqk_lo[:]), (t_wv[:], wv_hi[:], wv_lo[:]),
                  (t_w3, w3_hi[:], w3_lo[:]), (u_f[:], u_hi[:], u_lo[:]),
                  (t_w2g, w2_hi[:], w2_lo[:]),
                  (bank[0][:, 0:D], bw_hi[:], bw_lo[:])]
        TURNS = []
        for c in range(KD):
            TURNS += [(c, h, n_w1[:, h, c * N:(c + 1) * N]) for h in range(KH)]
        for c in range(KH):
            TURNS += [(2 + c // 2, 2 * (c % 2) + o, n_w2[:, o, c * N:(c + 1) * N]) for o in range(KD)]
        for c in range(2 * KD):
            TURNS += [(4 + c // 2, 2 * (c % 2) + o, n_w3[:, o, c * N:(c + 1) * N]) for o in range(KD)]
        for c in range(KD):
            TURNS += [(6, 2 * c + o, n_wv2[:, o, c * N:(c + 1) * N]) for o in range(KD)]
        for c in range(KD):
            TURNS += [(7, c, n_wqk[:, c * N:(c + 1) * N])]
        TURNED = [(t_w1[:, 0, :], bank[0][:, :]), (t_w1[:, 1, :], bank[1][:, :]),
                  (t_w2[:, 0:2, :], wide(2)), (t_w2[:, 2:4, :], wide(3)),
                  (t_w3[:, 0:2, :], wide(4)), (t_w3[:, 2:4, :], wide(5)),
                  (t_wv[:], wide(6)), (t_wqk[:], halves(7))]

        class Step:

            def __init__(self, i, u, counts=None, turns=None):
                self.i, self.u, self.counts, self.turns = i, u, counts, turns

            def on(self, lag):
                return self.counts is not None or 0 <= self.i - lag < PAIRS

            def had(self, lag):
                return self.counts is not None or 1 <= self.i - lag < PAIRS

            def n(self, lag):
                return self.i - lag + 1 if self.counts is None else self.counts[self.u - lag + 1]

            def before(self, lag):
                return self.n(lag + 1)

            def loads(self, lag):
                if self.counts is None:
                    return 32 * ((self.i - lag) // UNROLL + 1)
                return self.turns[(self.u - lag) // UNROLL]

            def slot(self, lag, slots):
                return (self.u - lag) % slots

        def steps(engine, step):
            for i in range(-1, UNROLL):
                step(Step(i, i % UNROLL))
            with engine.Fori(1, PAIRS // UNROLL - 1) as turn:
                counts = {c: engine.snap(turn * UNROLL + c) for c in range(-3, UNROLL + 3)}
                turns = [engine.snap((turn + 1) * 32), engine.snap((turn + 2) * 32)]
                for u in range(UNROLL):
                    step(Step(turn * UNROLL + u, u, counts, turns))
            for i in range(PAIRS - UNROLL, PAIRS + 3):
                step(Step(i, i % UNROLL))

        block = ctx.enter_context(nc.Block())

        @block.sync
        def _(sp):
            def load(dst, src, **more):
                sp.dma_start(dst, src, **more).then_inc(loaded, 16)

            def load_pair(slot, pair):
                sp.dma_start(a_in[:, slot], adj_pairs[pair]).then_inc(pair_loaded[slot], 16)
                sp.dma_start(x_in[:, slot], x_pairs[pair]).then_inc(pair_loaded[slot], 16)

            load_pair(0, 0)
            load(n_w1[:], l1_w1.rearrange("(c p) d -> p c d", p=N))
            load(n_w2[:], l1_w2.rearrange("(c p) d -> p c d", p=N))
            load(n_w3[:], l3_w.rearrange("(c p) d -> p c d", p=N))
            load(n_wv2[:], l2_wv.rearrange("(c p) d -> p c d", p=N))
            load(n_wqk[:], l2_wqk)
            load(gamma_t[:], l1_gamma.rearrange("(c p) -> p c", p=N), allow_slow_non_contiguous=True)
            load(beta_t[:], l1_beta.rearrange("(c p) -> p c", p=N), allow_slow_non_contiguous=True)
            load(n_wv0[:], l0_wv.rearrange("(c p) d -> p c d", p=N))
            load(aw_rows[:], l0_aw.rearrange("(h d) o -> (o h) d", h=2).partition_broadcast(N))
            load(bv_rows[:], l0_bv.partition_broadcast(N))
            load(ab_rows[:], l0_ab.partition_broadcast(N))
            for k in range(HOPS):
                load(n_wk[:, :, k, :], l0_wk[k].rearrange("(c p) d -> p c d", p=N))
            sp.wait_ge(zeroed, 1)
            for row in (0, 32):
                sp.dma_start(bias_f[row:row + HOPS, BK], l0_bk).then_inc(bias_in, 16)
                sp.dma_start(bias_f[row:row + 1, B1], l1_b1.unsqueeze(0)).then_inc(bias_in, 16)
                sp.dma_start(bias_f[row:row + 1, B2], l1_b2.unsqueeze(0)).then_inc(bias_in, 16)
            load_pair(1, 1)

            def step(s):
                if s.on(-2) and (s.counts is not None or s.i >= 0):
                    if s.on(2):
                        sp.wait_ge(x1_done, s.n(2))
                    load_pair(s.slot(-2, UNROLL), s.i + 2)
                if s.on(3):
                    sp.wait_ge(x4_done, s.n(3))
                    sp.dma_start(out_pairs[s.i - 3], x4[:]).then_inc(stored, 16)

            steps(sp, step)
            sp.wait_ge(stored, 16 * PAIRS)

        @block.tensor
        def _(pe):
            def product(dst, terms, bias=None):
                first = True
                if bias is not None:
                    pe.matmul(dst, ones_r[:], bias_r[:, bias], start=True, stop=False)
                    first = False
                for n, (lh, ll, rh, rl) in enumerate(terms):
                    pe.matmul(dst, lh, rh, start=first, stop=False)
                    pe.matmul(dst, lh, rl, start=False, stop=False)
                    last = pe.matmul(dst, ll, rh, start=False, stop=n == len(terms) - 1)
                    first = False
                return last

            pe.wait_ge(consts, 6)
            pe.wait_ge(loaded, 16 * 14)
            for b, n, block_in in TURNS:
                last = pe.transpose(bank[b][:, n * N:(n + 1) * N], block_in, ident[:])
            last.then_inc(turned, 1)
            pe.wait_ge(turned_sb, len(TURNED))
            for c in range(KH):
                last = pe.matmul(bank[0][:, 0:D], beta_t[:, c:c + 1].broadcast_to([N, N]),
                                 t_w2[:, c, :], start=c == 0, stop=c == KH - 1)
            last.then_inc(bw_ready, 1)
            pe.wait_ge(weights_ready, 1)

            def transposed(dst, src):
                for g in range(G):
                    for c in range(KD):
                        n = g * KD + c
                        last = pe.transpose(dst[:, n * N:(n + 1) * N], src[:, g, c * N:(c + 1) * N],
                                            ident[:])
                return last

            def times(hT, g, wt, cols=slice(None)):
                return [(hT[0][:, g * KD + c, :], hT[1][:, g * KD + c, :], wt[0][:, c, cols],
                         wt[1][:, c, cols]) for c in range(KD)]

            h0T, h2T, h3T, ph = (h0T_hi, h0T_lo), (h2T_hi, h2T_lo), (h3T_hi, h3T_lo), (ph_hi, ph_lo)

            def wk(hop):
                return wk_hi[:, :, hop], wk_lo[:, :, hop]

            def step(s):
                if s.on(0):
                    pe.wait_ge(normed_done[0], s.n(0))
                    transposed(h0T_ps, normed[0]).then_inc(h0T_ready, 1)
                if s.on(1):
                    pe.wait_ge(ptT_done, s.n(1))
                    pe.wait_ge(h1_hi_done, s.n(1))
                    pe.wait_ge(h1_lo_done, s.n(1))
                    p2 = s.slot(1, 2)
                    for g in range(G):
                        for c in range(KD):
                            n = g * KD + c
                            cols = slice(c * N, (c + 1) * N)
                            last = product(ph_ps[:, n * N:(n + 1) * N],
                                           [(h1_hi[:, g, cols], h1_lo[:, g, cols],
                                             pT_hi[:, p2, g], pT_lo[:, p2, g])])
                    last.then_inc(ph_ready, 1)
                if s.on(3):
                    pe.wait_ge(w_soft_done, s.n(3))
                    if s.had(3):
                        pe.wait_ge(x4_done, s.before(3))
                    for g in range(G):
                        last = product(v_ps[:, g], times(h2T, g, (wv_hi, wv_lo)))
                    last.then_inc(v_ready, 1)
                if s.on(0):
                    pe.wait_ge(a_mean_done, s.n(0))
                    a4 = s.slot(0, UNROLL)
                    for g in range(G):
                        pe.transpose(aT_ps[:, g], a_in[:, a4, g], ident[:])
                    for g in range(G):
                        last = pe.transpose(amT_ps[:, g], a_mean[:, g], ident[:])
                    last.then_inc(aT_ready, 1)
                    pe.wait_ge(h0T_done, s.n(0))
                    for g in range(G):
                        last = product(s_ps[:, g], times(h0T, g, (u_hi, u_lo)))
                    last.then_inc(s_ready, 1)
                    if s.had(0):
                        pe.wait_ge(x1_done, s.before(0))
                    for g in range(G):
                        last = product(y2_ps[:, g], times(h0T, g, wk(2)))
                    last.then_inc(y2_ready, 1)
                if s.on(1):
                    pe.wait_ge(ph_done, s.n(1))
                    if s.had(1):
                        pe.wait_ge(x2_done, s.before(1))
                    product(r_ps[0][:], times(ph, 0, (w1_hi, w1_lo)), B1).then_inc(r_ready[0], 1)
                if s.on(0):
                    pe.wait_ge(s_done, s.n(0))
                    for g in range(G):
                        last = pe.transpose(e_ps[:, g], s_sb[:, g, 0:1].broadcast_to([N, N]),
                                            ident[:])
                    last.then_inc(e_ready, 1)
                if s.on(3):
                    pe.wait_ge(normed_done[3], s.n(3))
                    transposed(h3T_ps, normed[3]).then_inc(h3T_ready, 1)
                if s.on(1):
                    product(r_ps[1][:], times(ph, 1, (w1_hi, w1_lo)), B1).then_inc(r_ready[1], 1)
                if s.on(0):
                    pe.wait_ge(binc_done, s.n(0))
                    pe.wait_ge(amT_done, s.n(0))
                    for g in range(G):
                        pe.matmul(node_ps[:, g:g + 1], inc_t[:, g], edge_w[:, g:g + 1],
                                  start=True, stop=True)
                    for g in range(G):
                        last = pe.matmul(gram_ps[:, g], inc_t[:, g], binc_t[:, g],
                                         start=True, stop=True)
                    last.then_inc(gram_ready, 1)
                if s.on(3):
                    pe.wait_ge(h3T_done, s.n(3))
                    product(zb_ps[:, 0], times(h3T, 0, (w3_hi[:, KD:], w3_lo[:, KD:])))
                if s.on(0):
                    pe.wait_ge(trans_done, s.n(0))
                    for g in range(G):
                        pe.transpose(tT_ps[:, g], trans[:, g], ident[:])
                    pe.wait_ge(prop_done, s.n(0))
                    for g in range(G):
                        last = pe.transpose(pT_ps[:, g], prop[:, g], ident[:])
                    last.then_inc(ptT_ready, 1)
                if s.on(2):
                    pe.wait_ge(normed_done[2], s.n(2))
                    transposed(h2T_ps, normed[2]).then_inc(h2T_ready, 1)
                if s.on(3):
                    product(zb_ps[:, 1], times(h3T, 1, (w3_hi[:, KD:], w3_lo[:, KD:])))\
                        .then_inc(zb_ready, 1)
                if s.on(0):
                    pe.wait_ge(ptT_done, s.n(0))
                    pe.wait_ge(y2_done, s.n(0))
                    t2 = s.slot(0, 2)
                    for g in range(G):
                        last = product(y1_ps[:, g], times(h0T, g, wk(1))
                                       + [(tT_hi[:, t2, g], tT_lo[:, t2, g], y2_hi[:, g], y2_lo[:, g])])
                    last.then_inc(y1_ready, 1)

                def conv2_in(g):
                    pe.wait_ge(rc_hi_done[g], s.n(1))
                    pe.wait_ge(rc_lo_done[g], s.n(1))
                    p2 = s.slot(1, 2)
                    for c in range(KH):
                        cols = slice(c * N, (c + 1) * N)
                        last = product(pr_ps[g][:, cols],
                                       [(rc_hi[:, g, cols], rc_lo[:, g, cols],
                                         pT_hi[:, p2, g], pT_lo[:, p2, g])])
                    last.then_inc(pr_ready[g], 1)

                if s.on(1):
                    conv2_in(0)
                if s.on(2):
                    pe.wait_ge(h2T_done, s.n(2))
                    for g in range(G):
                        last = product(qk_ps[:, g], times(h2T, g, (wqk_hi, wqk_lo)))
                    last.then_inc(qk_ready, 1)
                if s.on(3):
                    pe.wait_ge(zb_done, s.n(3))
                    a4 = s.slot(3, UNROLL)
                    for g in range(G):
                        last = product(out_ps[:, g], times(h3T, g, (w3_hi, w3_lo))
                                       + [(amT_hi[:, a4, g], amT_lo[:, a4, g],
                                           zb_hi[:, g], zb_lo[:, g])])
                    last.then_inc(out_ready, 1)
                if s.on(1):
                    conv2_in(1)
                if s.on(2):
                    pe.wait_ge(k_done, s.n(2))
                    a4 = s.slot(2, UNROLL)
                    for g in range(G):
                        last = product(ak_ps[:, g], [(amT_hi[:, a4, g], amT_lo[:, a4, g],
                                                      k_hi[:, g], k_lo[:, g])])
                    last.then_inc(ak_ready, 1)
                if s.on(0):
                    pe.wait_ge(y1_done, s.n(0))
                    t2 = s.slot(0, 2)
                    for g in range(G):
                        last = product(y0_ps[:, g], times(h0T, g, wk(0))
                                       + [(tT_hi[:, t2, g], tT_lo[:, t2, g], y1_hi[:, g], y1_lo[:, g])], BK)
                    last.then_inc(y0_ready, 1)
                if s.on(2):
                    pe.wait_ge(w_done, s.n(2))
                    if s.on(0):
                        pe.wait_ge(ptT_done, s.n(0))
                    for g in range(G):
                        last = pe.transpose(wrow_ps[:, g], w[:, g:g + 1].broadcast_to([N, N]),
                                            ident[:])
                    last.then_inc(wrow_ready, 1)
                if s.on(1):
                    p2 = s.slot(1, 2)
                    for g in range(G):
                        pe.wait_ge(pr_done[g], s.n(1))
                    for g in range(G):
                        last = product(conv_ps[:, g],
                                       [(pr_hi[:, g, c], pr_lo[:, g, c], w2_hi[:, c], w2_lo[:, c])
                                        for c in range(KH)]
                                       + [(pT_hi[:, p2, g], pT_lo[:, p2, g], bw_hi[:], bw_lo[:])], B2)
                    last.then_inc(conv_ready, 1)

            steps(pe, step)

        @block.scalar
        def _(act):
            def copy(dst, src, func=ACT.Copy):
                return nc.scalar.activation(dst, src, func)

            act.wait_ge(turned, 1)
            for dst, src in TURNED:
                copy(dst, src).then_inc(turned_sb, 1)
            act.wait_ge(bias_in, 16 * 6)
            copy(bias_r[:], bias_f[:]).then_inc(hi_ready, 1)
            act.wait_ge(turned_sb, len(TURNED))
            act.wait_ge(u_ready, 1)
            act.wait_ge(w2_scaled, 1)
            act.wait_ge(bw_ready, 1)
            for src, hi, _ in SPLITS:
                copy(hi, src).then_inc(hi_ready, 1)

            def step(s):
                if s.on(0):
                    act.wait_ge(h0T_ready, s.n(0))
                    copy(h0T_hi[:].rearrange("p n j -> p (n j)"), h0T_ps[:], ACT.Relu)\
                        .then_inc(h0T_hi_done, 1)
                if s.on(1):
                    act.wait_ge(ph_ready, s.n(1))
                    copy(ph_hi[:].rearrange("p n j -> p (n j)"), ph_ps[:]).then_inc(ph_hi_done, 1)
                if s.on(0):
                    act.wait_ge(aT_ready, s.n(0))
                    copy(amT_hi[:, s.slot(0, UNROLL)], amT_ps).then_inc(amT_hi_done, 1)
                    act.wait_ge(y2_ready, s.n(0))
                    copy(y2_hi[:], y2_ps).then_inc(y2_hi_done, 1)
                if s.on(1):
                    act.wait_ge(r_ready[0], s.n(1))
                    copy(r[:, 0], r_ps[0][:], ACT.Relu).then_inc(r_done[0], 1)
                if s.on(0):
                    act.wait_ge(leaky_done, s.n(0))
                    copy(z_exp[:], z_leaky[:], ACT.Exp).then_inc(exp_done, 1)
                if s.on(3):
                    act.wait_ge(h3T_ready, s.n(3))
                    copy(h3T_hi[:].rearrange("p n j -> p (n j)"), h3T_ps[:], ACT.Relu)\
                        .then_inc(h3T_hi_done, 1)
                if s.on(1):
                    act.wait_ge(r_ready[1], s.n(1))
                    copy(r[:, 1], r_ps[1][:], ACT.Relu).then_inc(r_done[1], 1)
                if s.on(0):
                    act.wait_ge(node_inv_done, s.n(0))
                    for g in range(G):
                        last = nc.scalar.activation(prop[:, g], gram_ps[:, g], ACT.Copy,
                                                    scale=node_inv[:, g:g + 1])
                    last.then_inc(prop_done, 1)
                    act.wait_ge(ptT_ready, s.n(0))
                    copy(ptT_hi[:, s.slot(0, 2)].rearrange("p k g n -> p (k g n)"), bank[2][:])\
                        .then_inc(ptT_hi_done, 1)
                if s.on(1):
                    act.wait_ge(rc_done[0], s.n(1))
                    copy(rc_hi[:, 0], rc[:, 0]).then_inc(rc_hi_done[0], 1)
                if s.on(2):
                    act.wait_ge(h2T_ready, s.n(2))
                    copy(h2T_hi[:].rearrange("p n j -> p (n j)"), h2T_ps[:], ACT.Relu)\
                        .then_inc(h2T_hi_done, 1)
                if s.on(3):
                    act.wait_ge(zb_ready, s.n(3))
                    copy(zb_hi[:], zb_ps).then_inc(zb_hi_done, 1)
                if s.on(1):
                    act.wait_ge(rc_done[1], s.n(1))
                    copy(rc_hi[:, 1], rc[:, 1]).then_inc(rc_hi_done[1], 1)
                if s.on(0):
                    act.wait_ge(y1_ready, s.n(0))
                    copy(y1_hi[:], y1_ps).then_inc(y1_hi_done, 1)
                if s.on(1):
                    act.wait_ge(pr_ready[0], s.n(1))
                    copy(pr_hi[:, 0].rearrange("p c j -> p (c j)"), pr_ps[0][:])\
                        .then_inc(pr_hi_done[0], 1)
                if s.on(2):
                    act.wait_ge(qk_ready, s.n(2))
                    copy(k_hi[:], qk_ps[:, :, ATT:])
                    copy(q_sb[:], qk_ps[:, :, :ATT]).then_inc(q_done, 1)
                if s.on(1):
                    act.wait_ge(pr_ready[1], s.n(1))
                    copy(pr_hi[:, 1].rearrange("p c j -> p (c j)"), pr_ps[1][:])\
                        .then_inc(pr_hi_done[1], 1)
                if s.on(2):
                    act.wait_ge(w_nmax_done, s.n(2))
                    for g in range(G):
                        nc.scalar.activation(w_junk[:, g], wrow_ps[:, g], ACT.Exp,
                                             bias=w_nmax[:, g:g + 1], accum_out=w_sum[:, g:g + 1])
                    for g in range(G):
                        last = nc.scalar.activation(w_exp[:, g:g + 1], w[:, g:g + 1], ACT.Exp,
                                                    bias=w_nmax[:, g:g + 1])
                    last.then_inc(w_exp_done, 1)
                if s.on(0):
                    act.wait_ge(normed_done[1], s.n(0))
                    copy(h1[:], normed[1][:], ACT.Relu).then_inc(h1_done, 1)
                    copy(h1_hi[:], normed[1][:], ACT.Relu).then_inc(h1_hi_done, 1)

            steps(act, step)

        @block.vector
        def _(dve):
            def rest(dst, src, hi):
                return dve.tensor_tensor(dst, src, hi.bitcast(F32), ALU.subtract)

            def relu_rest(dst, src, hi):
                return dve.scalar_tensor_tensor(out=dst, in0=src, scalar=0.0, in1=hi.bitcast(F32),
                                                op0=ALU.max, op1=ALU.subtract)

            dve.wait_ge(loaded, 16 * 14)
            n = 0
            for c in range(KD):
                for h in range(2):
                    n += 1
                    dve.scalar_tensor_tensor(out=junk[:], in0=n_wv0[:, c], scalar=1.0,
                                             in1=aw_rows[:, h], op0=ALU.mult, op1=ALU.mult,
                                             accum_out=u_f[:, c, h:h + 1]).then_inc(kappa_ready, 1)
                    dve.wait_ge(kappa_ready, n)
            for h in range(2):
                n += 1
                last = dve.scalar_tensor_tensor(out=junk[:], in0=bv_rows[:], scalar=1.0,
                                                in1=aw_rows[:, h], op0=ALU.mult, op1=ALU.mult,
                                                accum_out=kappa[:, h:h + 1])
                last.then_inc(kappa_ready, 1)
                dve.wait_ge(kappa_ready, n)
            dve.tensor_tensor(kappa1[:], kappa[:, 0:1], kappa[:, 1:2], ALU.add)\
               .then_inc(kappa_ready, 1)
            dve.wait_ge(kappa_ready, n + 1)
            dve.tensor_scalar(s_const[:], kappa1[:], ab_rows[:, 0:1], 0.5, ALU.add, ALU.mult)\
               .then_inc(u_ready, 1)
            dve.wait_ge(turned_sb, 4)
            for c in range(KH):
                last = dve.tensor_scalar(t_w2g[:, c], t_w2[:, c], gamma_t[:, c:c + 1], None,
                                         ALU.mult)
            last.then_inc(w2_scaled, 1)
            dve.wait_ge(hi_ready, 1)
            rest(bias_r[32:64], bias_f[32:64], bias_r[32:64])
            dve.wait_ge(u_ready, 1)
            dve.wait_ge(w2_scaled, 1)
            for n, (src, hi, lo) in enumerate(SPLITS):
                dve.wait_ge(hi_ready, n + 2)
                last = rest(lo, src, hi)
            last.then_inc(weights_ready, 1)

            def norm_stats(layer, src, count):
                for g in range(G):
                    last = dve.bn_stats(stats[layer][:, g], src[:, g])
                last.then_inc(stats_done[layer], 1)
                dve.wait_ge(stats_done[layer], count)
                dve.memset(held[:], 0.0)
                for g in range(G):
                    last = dve.bn_aggr(moments[layer][:, g], stats[layer][:, g])
                last.then_inc(moments_done[layer], 1)

            def norm(layer, src, count):
                dve.wait_ge(rstd_done[layer], count)
                for g in range(G):
                    last = dve.tensor_scalar(normed[layer][:, g], src[:, g],
                                             moments[layer][:, g, 0:1], rstd[layer][:, g:g + 1],
                                             ALU.subtract, ALU.mult)
                last.then_inc(normed_done[layer], 1)

            def r_stats(s, g):
                dve.wait_ge(r_done[g], s.n(1))
                dve.bn_stats(stats[4][:, g], r[:, g]).then_inc(r_stats_done[g], 1)
                dve.wait_ge(r_stats_done[g], s.n(1))
                dve.memset(held[:], 0.0)
                dve.bn_aggr(moments[4][:, g], stats[4][:, g]).then_inc(r_moments_done[g], 1)

            def r_norm(s, g):
                dve.wait_ge(r_rstd_done[g], s.n(1))
                dve.tensor_scalar(rc[:, g], r[:, g], moments[4][:, g, 0:1], rstd[4][:, g:g + 1],
                                  ALU.subtract, ALU.mult).then_inc(rc_done[g], 1)

            def step(s):
                if s.on(0):
                    dve.wait_ge(h0T_hi_done, s.n(0))
                    relu_rest(h0T_lo[:].rearrange("p n j -> p (n j)"), h0T_ps[:],
                              h0T_hi[:].rearrange("p n j -> p (n j)")).then_inc(h0T_done, 1)
                if s.on(1):
                    dve.wait_ge(ph_hi_done, s.n(1))
                    rest(ph_lo[:].rearrange("p n j -> p (n j)"), ph_ps[:],
                         ph_hi[:].rearrange("p n j -> p (n j)")).then_inc(ph_done, 1)
                if s.on(3):
                    dve.wait_ge(v_ready, s.n(3))
                    for g in range(G):
                        last = dve.scalar_tensor_tensor(out=x3[:, g], in0=v_ps[:, g],
                                                        scalar=w_soft[:, g:g + 1],
                                                        in1=x2[:, s.slot(3, 2), g],
                                                        op0=ALU.mult, op1=ALU.add)
                    last.then_inc(x3_done, 1)
                if s.on(0):
                    dve.wait_ge(amT_hi_done, s.n(0))
                    dve.tensor_scalar(inc_t[:], aT_ps, 0.0, None, ALU.not_equal)\
                       .then_inc(inc_done, 1)
                    dve.tensor_copy(edge_w[:], aT_ps[:, :, 0:1].rearrange("p g o -> p (g o)"))
                    dve.wait_ge(inc_done, s.n(0))
                    dve.tensor_reduce(edge_cnt[:], inc_t[:], AX_X, ALU.add)\
                       .then_inc(edge_cnt_done, 1)
                    dve.wait_ge(edge_cnt_done, s.n(0))
                    dve.tensor_scalar(edge_cnt1[:], edge_cnt[:], 1.0, None, ALU.max)\
                       .then_inc(edge_cnt1_done, 1)
                    dve.wait_ge(edge_cnt1_done, s.n(0))
                    dve.reciprocal(edge_inv[:], edge_cnt1[:]).then_inc(edge_inv_done, 1)
                if s.on(3):
                    dve.wait_ge(x3_done, s.n(3))
                    norm_stats(3, x3, s.n(3))
                if s.on(0):
                    dve.wait_ge(s_ready, s.n(0))
                    dve.tensor_scalar(s_sb[:], s_ps, s_const[:, 0:1], None, ALU.add)\
                       .then_inc(s_done, 1)
                    rest(amT_lo[:, s.slot(0, UNROLL)], amT_ps, amT_hi[:, s.slot(0, UNROLL)])\
                        .then_inc(amT_done, 1)
                if s.on(3):
                    norm(3, x3, s.n(3))
                if s.on(0):
                    dve.wait_ge(y2_hi_done, s.n(0))
                    rest(y2_lo[:], y2_ps, y2_hi[:]).then_inc(y2_done, 1)
                if s.on(2):
                    dve.wait_ge(x2_done, s.n(2))
                    norm_stats(2, x2[:, s.slot(2, 2)], s.n(2))
                if s.on(0):
                    dve.wait_ge(e_ready, s.n(0))
                    dve.tensor_tensor(z[:], e_ps, s_sb[:, :, 1:2].broadcast_to([N, G, N]), ALU.add)\
                       .then_inc(z_done, 1)
                    dve.wait_ge(z_done, s.n(0))
                    dve.scalar_tensor_tensor(out=z_leaky[:], in0=z[:], scalar=SLOPE, in1=z[:],
                                             op0=ALU.mult, op1=ALU.max).then_inc(leaky_done, 1)
                if s.on(1):
                    r_stats(s, 0)
                if s.on(3):
                    dve.wait_ge(h3T_hi_done, s.n(3))
                    relu_rest(h3T_lo[:].rearrange("p n j -> p (n j)"), h3T_ps[:],
                              h3T_hi[:].rearrange("p n j -> p (n j)")).then_inc(h3T_done, 1)
                if s.on(0):
                    dve.wait_ge(exp_done, s.n(0))
                    for g in range(G):
                        last = dve.scalar_tensor_tensor(out=alpha[:, g], in0=z_exp[:, g], scalar=1.0,
                                                        in1=a_in[:, s.slot(0, UNROLL), g],
                                                        op0=ALU.mult, op1=ALU.mult,
                                                        accum_out=row_sum[:, g:g + 1])
                    last.then_inc(alpha_done, 1)
                    dve.wait_ge(alpha_done, s.n(0))
                    dve.tensor_scalar(row_sum1[:], row_sum[:], ROW_EPS, None, ALU.add)\
                       .then_inc(row_sum_done, 1)
                    dve.wait_ge(row_sum_done, s.n(0))
                    dve.reciprocal(row_inv[:], row_sum1[:]).then_inc(row_inv_done, 1)
                    dve.wait_ge(gram_ready, s.n(0))
                    dve.tensor_scalar(node_w1[:], node_ps, TINY, None, ALU.max)\
                       .then_inc(node_w1_done, 1)
                    dve.wait_ge(node_w1_done, s.n(0))
                    dve.reciprocal(node_w2[:], node_w1[:]).then_inc(node_w2_done, 1)
                    dve.wait_ge(node_w2_done, s.n(0))
                    dve.scalar_tensor_tensor(out=node_inv[:], in0=node_ps, scalar=0.0,
                                             in1=node_w2[:], op0=ALU.is_gt, op1=ALU.mult)\
                       .then_inc(node_inv_done, 1)
                if s.on(1):
                    r_norm(s, 0)
                if s.on(2):
                    norm(2, x2[:, s.slot(2, 2)], s.n(2))
                if s.on(1):
                    r_stats(s, 1)
                if s.on(0):
                    dve.wait_ge(ptT_hi_done, s.n(0))
                    rest(ptT_lo[:, s.slot(0, 2)].rearrange("p k g n -> p (k g n)"), bank[2][:],
                         ptT_hi[:, s.slot(0, 2)].rearrange("p k g n -> p (k g n)"))\
                        .then_inc(ptT_done, 1)
                if s.on(1):
                    r_norm(s, 1)
                if s.on(2):
                    dve.wait_ge(h2T_hi_done, s.n(2))
                    relu_rest(h2T_lo[:].rearrange("p n j -> p (n j)"), h2T_ps[:],
                              h2T_hi[:].rearrange("p n j -> p (n j)")).then_inc(h2T_done, 1)
                if s.on(3):
                    dve.wait_ge(zb_hi_done, s.n(3))
                    rest(zb_lo[:], zb_ps, zb_hi[:]).then_inc(zb_done, 1)
                if s.on(0):
                    dve.wait_ge(y1_hi_done, s.n(0))
                    rest(y1_lo[:], y1_ps, y1_hi[:]).then_inc(y1_done, 1)
                if s.on(1):
                    dve.wait_ge(pr_hi_done[0], s.n(1))
                    rest(pr_lo[:, 0].rearrange("p c j -> p (c j)"), pr_ps[0][:],
                         pr_hi[:, 0].rearrange("p c j -> p (c j)")).then_inc(pr_done[0], 1)
                if s.on(2):
                    dve.wait_ge(q_done, s.n(2))
                    rest(k_lo[:], qk_ps[:, :, ATT:], k_hi[:]).then_inc(k_done, 1)
                if s.on(3):
                    dve.wait_ge(out_ready, s.n(3))
                    if s.had(3):
                        dve.wait_ge(stored, 16 * s.before(3))
                    dve.scalar_tensor_tensor(out=x4[:], in0=out_ps, scalar=0.0, in1=x3[:],
                                             op0=ALU.max, op1=ALU.add).then_inc(x4_done, 1)
                if s.on(1):
                    dve.wait_ge(pr_hi_done[1], s.n(1))
                    rest(pr_lo[:, 1].rearrange("p c j -> p (c j)"), pr_ps[1][:],
                         pr_hi[:, 1].rearrange("p c j -> p (c j)")).then_inc(pr_done[1], 1)
                if s.on(2):
                    dve.wait_ge(ak_ready, s.n(2))
                    for g in range(G):
                        last = dve.scalar_tensor_tensor(out=qk_junk[:, g], in0=ak_ps[:, g],
                                                        scalar=w_scale[:, s.slot(2, UNROLL), g:g + 1],
                                                        in1=q_sb[:, g], op0=ALU.mult, op1=ALU.mult,
                                                        accum_out=w[:, g:g + 1])
                    last.then_inc(w_done, 1)
                if s.on(0):
                    dve.wait_ge(y0_ready, s.n(0))
                    dve.scalar_tensor_tensor(out=x1[:], in0=y0_ps, scalar=0.0,
                                             in1=x_in[:, s.slot(0, UNROLL)],
                                             op0=ALU.max, op1=ALU.add).then_inc(x1_done, 1)
                    dve.wait_ge(x1_done, s.n(0))
                    norm_stats(1, x1, s.n(0))
                if s.on(2):
                    dve.wait_ge(wrow_ready, s.n(2))
                    dve.tensor_reduce(w_nmax[:], wrow_ps, AX_X, ALU.max, negate=True)\
                       .then_inc(w_nmax_done, 1)
                if s.on(-1):
                    nxt = s.slot(-1, UNROLL)
                    dve.wait_ge(pair_loaded[nxt], s.loads(-1))
                    dve.tensor_reduce(deg[:], a_in[:, nxt], AX_X, ALU.add).then_inc(deg_done, 1)
                    dve.wait_ge(deg_done, s.n(-1))
                    dve.tensor_scalar(deg_max[:], deg[:], DEG_EPS, None, ALU.max)\
                       .then_inc(deg_max_done, 1)
                    dve.wait_ge(deg_max_done, s.n(-1))
                    dve.reciprocal(deg_inv[:], deg_max[:]).then_inc(deg_inv_done, 1)
                    dve.tensor_scalar(w_scale[:, nxt], deg_max[:], float(ATT) ** -0.5, None,
                                      ALU.mult)
                    norm_stats(0, x_in[:, nxt], s.n(-1))
                if s.on(0):
                    norm(1, x1, s.n(0))
                if s.on(-1):
                    norm(0, x_in[:, s.slot(-1, UNROLL)], s.n(-1))
                if s.on(2):
                    dve.wait_ge(w_exp_done, s.n(2))
                    dve.reciprocal(w_inv[:], w_sum[:]).then_inc(w_inv_done, 1)
                    dve.wait_ge(w_inv_done, s.n(2))
                    dve.tensor_tensor(w_soft[:], w_exp[:], w_inv[:], ALU.mult)\
                       .then_inc(w_soft_done, 1)
                if s.on(1):
                    dve.wait_ge(conv_ready, s.n(1))
                    dve.wait_ge(xh_done, s.n(1))
                    dve.tensor_tensor(x2[:, s.slot(1, 2)], conv_ps, xh[:, s.slot(1, 2)], ALU.add)\
                       .then_inc(x2_done, 1)

            steps(dve, step)

        @block.gpsimd
        def _(pool):
            pool.memset(bias_f[:], 0.0).then_inc(zeroed, 1)
            pool.memset(ones_r[:].bitcast(F32), 1.0).then_inc(consts, 1)
            pool.memset(eps_ln[:], LN_EPS).then_inc(consts, 1)
            pool.memset(minus_half[:], -0.5).then_inc(consts, 1)
            pool.memset(ident[:], 0.0).then_inc(consts, 1)
            pool.wait_ge(consts, 4)
            pool.affine_select(out=ident[:], in_=ident[:], compare_op=ALU.not_equal, fill=1.0, base=0,
                               pattern=[[-1, N]], channel_multiplier=1).then_inc(consts, 2)
            pool.wait_ge(consts, 6)

            def inverse_std(layer, count):
                pool.wait_ge(moments_done[layer], count)
                pool.tensor_tensor(var_eps[layer][:], moments[layer][:, :, 1], eps_ln[:], ALU.add)\
                    .then_inc(var_done[layer], 1)
                pool.wait_ge(var_done[layer], count)
                pool.tensor_tensor(rstd[layer][:], var_eps[layer][:], minus_half[:], ALU.pow)\
                    .then_inc(rstd_done[layer], 1)

            def r_inverse_std(s, g):
                pool.wait_ge(r_moments_done[g], s.n(1))
                pool.tensor_tensor(var_eps[4][:, g:g + 1], moments[4][:, g, 1:2],
                                   eps_ln[:, g:g + 1], ALU.add).then_inc(r_var_done[g], 1)
                pool.wait_ge(r_var_done[g], s.n(1))
                pool.tensor_tensor(rstd[4][:, g:g + 1], var_eps[4][:, g:g + 1],
                                   minus_half[:, g:g + 1], ALU.pow).then_inc(r_rstd_done[g], 1)

            def r_rest(s, g):
                pool.wait_ge(rc_hi_done[g], s.n(1))
                pool.tensor_tensor(rc_lo[:, g], rc[:, g], rc_hi[:, g].bitcast(F32), ALU.subtract)\
                    .then_inc(rc_lo_done[g], 1)

            def rows(v):
                return v.unsqueeze(2).broadcast_to([N, G, N])

            def step(s):
                if s.on(0):
                    pool.wait_ge(edge_inv_done, s.n(0))
                    pool.tensor_tensor(binc_t[:], inc_t[:], rows(edge_inv[:]), ALU.mult)\
                        .then_inc(binc_done, 1)
                if s.on(3):
                    inverse_std(3, s.n(3))
                if s.on(2):
                    inverse_std(2, s.n(2))
                if s.on(1):
                    r_inverse_std(s, 0)
                if s.on(0):
                    pool.wait_ge(row_inv_done, s.n(0))
                    pool.tensor_tensor(trans[:], alpha[:], rows(row_inv[:]), ALU.mult)\
                        .then_inc(trans_done, 1)
                if s.on(1):
                    r_inverse_std(s, 1)
                    r_rest(s, 0)
                    r_rest(s, 1)
                if s.on(0):
                    inverse_std(1, s.n(0))
                if s.on(-1):
                    pool.wait_ge(deg_inv_done, s.n(-1))
                    pool.tensor_tensor(a_mean[:], a_in[:, s.slot(-1, UNROLL)], rows(deg_inv[:]),
                                       ALU.mult).then_inc(a_mean_done, 1)
                    inverse_std(0, s.n(-1))
                if s.on(0):
                    pool.wait_ge(h1_hi_done, s.n(0))
                    pool.tensor_tensor(h1_lo[:], h1[:], h1_hi[:].bitcast(F32), ALU.subtract)\
                        .then_inc(h1_lo_done, 1)
                    pool.tensor_tensor(xh[:, s.slot(0, 2)], x1[:], h1[:], ALU.add)\
                        .then_inc(xh_done, 1)

            steps(pool, step)


_INS = ['x', 'adj', 'L0_gnn_Wv', 'L0_gnn_bv', 'L0_gnn_aw', 'L0_gnn_ab', 'L0_gnn_Wk', 'L0_gnn_bk',
        'L1_gnn_W1', 'L1_gnn_b1', 'L1_gnn_gamma', 'L1_gnn_beta', 'L1_gnn_W2', 'L1_gnn_b2',
        'L2_gnn_W_qk', 'L2_gnn_W_v', 'L3_gnn_W']


def kernel(**inputs):
    import numpy as np
    import concourse.bacc as bacc
    from concourse.bass_utils import run_bass_kernel_spmd

    nc = bacc.Bacc("TRN2", target_bir_lowering=False, num_devices=1)
    arrays, args = {}, []
    for name in _INS:
        a = np.ascontiguousarray(inputs[name])
        arrays[f"in_{name}"] = a
        args.append(nc.dram_tensor(f"in_{name}", a.shape, mybir.dt.from_np(a.dtype),
                                   kind="ExternalInput").ap())
    out = nc.dram_tensor("out_x", inputs["x"].shape, F32, kind="ExternalOutput").ap()
    build_program(nc, *args, out)
    result = run_bass_kernel_spmd(nc, [arrays], core_ids=[0])
    return result.results[0]["out_x"]
```

```python
from contextlib import ExitStack

import concourse.bass as bass
from concourse import mybir

F32 = mybir.dt.float32
F32R = mybir.dt.float32r
ALU = mybir.AluOpType
ACT = mybir.ActivationFunctionType
AX_X = mybir.AxisListType.X

LN_EPS = 1e-5
ROW_EPS = 1e-12
DEG_EPS = 1e-6
SLOPE = 0.2
TINY = 1e-38
UNROLL = 4


def build_program(nc, x, adj, l0_wv, l0_bv, l0_aw, l0_ab, l0_wk, l0_bk, l1_w1, l1_b1, l1_gamma,
                  l1_beta, l1_w2, l1_b2, l2_wqk, l2_wv, l3_w, out):
    graphs, N, D = x.shape
    G = 2
    PAIRS = graphs // G
    KD = D // N
    HID = l1_w1.shape[0]
    KH = HID // N
    ATT = l2_wqk.shape[0] // 2
    HOPS = l0_wk.shape[0]
    assert N == 128 and D == 256 and HID == 512 and HOPS == 3 and ATT == 64 and PAIRS % UNROLL == 0

    x_pairs = x.rearrange("(p g) n d -> p n g d", g=G)
    adj_pairs = adj.rearrange("(p g) i j -> p i g j", g=G)
    out_pairs = out.rearrange("(p g) n d -> p n g d", g=G)

    with ExitStack() as ctx:
        def sb(name, shape, dt=F32):
            return ctx.enter_context(nc.sbuf_tensor(name, shape, dt))

        def sem(name):
            return ctx.enter_context(nc.semaphore(name))

        def split(name, shape):
            return sb(name + "_hi", shape, F32R), sb(name + "_lo", shape, F32R)

        ident = sb("ident", [N, N])
        ones_r = sb("ones_r", [N, N], F32R)
        eps_ln = sb("eps_ln", [N, G])
        minus_half = sb("minus_half", [N, G])
        s_const = sb("s_const", [N, 1])
        wk_hi, wk_lo = split("wk", [N, KD, HOPS * D + 2])
        w1_hi, w1_lo = split("w1", [N, KD, HID])
        w2_hi, w2_lo = split("w2", [N, KH, D])
        wqkv_hi, wqkv_lo = split("wqkv", [N, KD, 2 * ATT + D])
        w3_hi, w3_lo = split("w3", [N, 2 * KD, D])
        b2_rows = sb("b2_rows", [N, D])
        BK, B1, BW = slice(0, D), slice(D, D + HID), slice(D + HID, 2 * D + HID)
        bias_f = sb("bias_f", [N, 2 * D + HID])
        bias_r = sb("bias_r", [N, 2 * D + HID], F32R)

        n_w2 = sb("n_w2", [N, KD, HID])
        n_wqk = sb("n_wqk", [N, D])
        n_w3 = sb("n_w3", [N, KD, 2 * D])
        bv_rows = sb("bv_rows", [N, D])
        ab_rows = sb("ab_rows", [N, 1])
        gamma_t = sb("gamma_t", [N, KH])
        beta_t = sb("beta_t", [N, KH])
        kappa = sb("kappa", [N, 2])
        kappa1 = sb("kappa1", [N, 1])
        junk = sb("junk", [N, D])
        t_wqk = sb("t_wqk", [N, KD, 2 * ATT])

        x_in = sb("x_in", [N, UNROLL, G, D])
        a_in = sb("a_in", [N, UNROLL, G, N])
        deg = sb("deg", [N, G])
        deg_max = sb("deg_max", [N, G])
        deg_inv = sb("deg_inv", [N, G])
        w_scale = sb("w_scale", [N, UNROLL, G])
        a_mean = sb("a_mean", [N, G, N])
        amT_hi, amT_lo = split("amT", [N, UNROLL, G, N])
        inc_t = sb("inc_t", [N, G, N], F32R)
        edge_cnt = sb("edge_cnt", [N, G])
        edge_cnt1 = sb("edge_cnt1", [N, G])
        edge_inv = sb("edge_inv", [N, G])
        einv_hi, einv_lo = split("einv", [N, G])
        binc_hi, binc_lo = split("binc", [N, G, N + 2])
        node_w1 = sb("node_w1", [N, G, 1])
        node_w2 = sb("node_w2", [N, G, 1])
        node_inv = sb("node_inv", [N, G, 1])
        prop = sb("prop", [N, G, N])
        ptT_hi, ptT_lo = split("ptT", [N, 2, 2, G, N])
        stats = [sb(f"stats{n}", [N, G, 6]) for n in range(5)]
        moments = [sb(f"moments{n}", [N, G, 2]) for n in range(5)]
        var_eps = [sb(f"var_eps{n}", [N, G]) for n in range(5)]
        rstd = [sb(f"rstd{n}", [N, G]) for n in range(5)]
        normed = [sb(f"normed{n}", [N, G, D]) for n in range(4)]
        held = sb("held", [N, 1])

        h0T_hi, h0T_lo = split("h0T", [N, G * KD, N])
        s_sb = sb("s_sb", [N, G, 2])
        y2_hi, y2_lo = split("y2", [N, G, D])
        y1_hi, y1_lo = split("y1", [N, G, D])
        z = sb("z", [N, G, N])
        z_leaky = sb("z_leaky", [N, G, N])
        z_exp = sb("z_exp", [N, G, N])
        alpha = sb("alpha", [N, G, N])
        row_sum = sb("row_sum", [N, G])
        row_sum1 = sb("row_sum1", [N, G])
        row_inv = sb("row_inv", [N, G])
        trans = sb("trans", [N, G, N])
        x1 = sb("x1", [N, G, D])

        h1 = sb("h1", [N, G, D])
        h1_hi, h1_lo = split("h1", [N, G, D])
        x1b = sb("x1b", [N, G, D])
        xh = sb("xh", [N, 2, G, D])
        ph_hi, ph_lo = split("ph", [N, G * KD, N])
        r = sb("r", [N, G, HID])
        rc = sb("rc", [N, G, HID])
        rcT_hi, rcT_lo = split("rcT", [N, G, KH, N])
        yp_hi, yp_lo = split("yp", [N, G, D])
        x2 = sb("x2", [N, 2, G, D])

        h2T_hi, h2T_lo = split("h2T", [N, G * KD, N])
        q_sb = sb("q_sb", [N, G, ATT])
        k_hi, k_lo = split("k", [N, G, ATT])
        v_sb = sb("v_sb", [N, 2, G, D])
        qk_junk = sb("qk_junk", [N, G, ATT])
        w = sb("w", [N, G])
        w_nmax = sb("w_nmax", [N, G])
        w_junk = sb("w_junk", [N, G, N])
        w_sum = sb("w_sum", [N, G])
        w_exp = sb("w_exp", [N, G])
        w_inv = sb("w_inv", [N, G])
        w_soft = sb("w_soft", [N, G])
        x3 = sb("x3", [N, 2, G, D])

        h3T_hi, h3T_lo = split("h3T", [N, G * KD, N])
        zb_hi, zb_lo = split("zb", [N, G, D])
        x4_relu = sb("x4_relu", [N, G, D])
        x4 = sb("x4", [N, G, D])

        n_wv0, n_wv2, aw_rows = normed[1], normed[2], normed[3]
        n_w1 = v_sb[:].rearrange("p s g d -> p (s g) d")
        t_w1 = r
        t_w2 = rc[:].rearrange("p g (c d) -> p (g c) d", d=D)
        t_w2g = xh[:].rearrange("p s g d -> p (s g) d")
        t_w3 = x2[:].rearrange("p s g d -> p (s g) d")
        t_wv = x3[:, 0]
        wk_f = sb("wk_f", [N, KD, HOPS * D + 2])
        bw_hi = sb("bw_hi", [N, D], F32R)

        psum = ctx.enter_context(nc.psum_tensor("psum", [N, 8, 512], F32))

        def whole(b):
            return psum[:, b, :]

        def halves(b, first=0):
            return psum[:, b, first:first + G * N].rearrange("p (g n) -> p g n", g=G)

        def wide(b):
            return psum[:, b, :].rearrange("p (g d) -> p g d", g=G)

        h0T_ps, wrow_ps, rcT1_ps = whole(0), halves(0), whole(0)
        h3T_ps, zb_ps = whole(1), wide(1)
        y2_ps, s_ps = psum[:, 1:3, 0:D], psum[:, 1:3, D:D + 2]
        r1_ps, y0_ps, ph_ps = whole(2), wide(2), whole(2)
        y1_ps, out_ps = wide(3), wide(3)
        r0_ps, h2T_ps, rcT0_ps, e_ps = whole(4), whole(4), whole(4), halves(4)
        aT_ps, amT_ps = halves(5), halves(5, G * N)
        gram_ps = psum[:, 5, 0:G * (N + 2)].rearrange("p (g n) -> p g n", g=G)
        qkv_ps = psum[:, 6:8, 0:2 * ATT + D]
        ak_ps = psum[:, 6, 0:G * ATT].rearrange("p (g a) -> p g a", g=G)
        conv_ps = wide(6)
        pT_ps, tT_ps, ptT_ps = halves(7), halves(7, G * N), whole(7)
        yp_ps = wide(7)
        r_ps, rcT_ps = [r0_ps, r1_ps], [rcT0_ps, rcT1_ps]

        zeroed = sem("zeroed")
        consts = sem("consts")
        loaded = sem("loaded")
        bias_in = sem("bias_in")
        turned = sem("turned")
        turned_sb = sem("turned_sb")
        w2_scaled = sem("w2_scaled")
        bw_ready = sem("bw_ready")
        kappa_ready = sem("kappa_ready")
        u_ready = sem("u_ready")
        hi_ready = sem("hi_ready")
        bw_rows = sem("bw_rows")
        weights_ready = sem("weights_ready")

        pair_loaded = [sem(f"pair_loaded{k}") for k in range(UNROLL)]
        stored = sem("stored")
        stats_done, moments_done, var_done, rstd_done, normed_done = (
            [sem(f"{name}_done{n}") for n in range(4)]
            for name in ("stats", "moments", "var", "rstd", "normed"))
        r_stats_done, r_moments_done, r_var_done, r_rstd_done = (
            [sem(f"{name}_done{g}") for g in range(G)]
            for name in ("r_stats", "r_moments", "r_var", "r_rstd"))
        deg_done, deg_max_done, deg_inv_done = sem("deg_done"), sem("deg_max_done"), sem("deg_inv_done")
        a_mean_done = sem("a_mean_done")
        aT_ready, amT_hi_done, amT_done = sem("aT_ready"), sem("amT_hi_done"), sem("amT_done")
        inc_done, edge_w_done, edge_cnt_done = sem("inc_done"), sem("edge_w_done"), sem("edge_cnt_done")
        edge_cnt1_done, edge_inv_done = sem("edge_cnt1_done"), sem("edge_inv_done")
        einv_hi_done, einv_done = sem("einv_hi_done"), sem("einv_done")
        binc_done = sem("binc_done")
        gram_ready = sem("gram_ready")
        node_w1_done, node_w2_done = sem("node_w1_done"), sem("node_w2_done")
        node_inv_done = sem("node_inv_done")
        prop_done = sem("prop_done")
        ptT_ready, ptT_hi_done, ptT_done = sem("ptT_ready"), sem("ptT_hi_done"), sem("ptT_done")

        h0T_ready, h0T_hi_done, h0T_done = sem("h0T_ready"), sem("h0T_hi_done"), sem("h0T_done")
        y2_ready, y2_hi_done, y2_done = sem("y2_ready"), sem("y2_hi_done"), sem("y2_done")
        s_done = sem("s_done")
        e_ready, z_done, leaky_done, exp_done = sem("e_ready"), sem("z_done"), sem("leaky_done"), sem("exp_done")
        alpha_done, row_sum_done, row_inv_done = sem("alpha_done"), sem("row_sum_done"), sem("row_inv_done")
        trans_done = sem("trans_done")
        y1_ready, y1_hi_done, y1_done = sem("y1_ready"), sem("y1_hi_done"), sem("y1_done")
        y0_ready, x1_done = sem("y0_ready"), sem("x1_done")

        h1_done, h1_hi_done, h1_lo_done = sem("h1_done"), sem("h1_hi_done"), sem("h1_lo_done")
        x1b_done, xh_done = sem("x1b_done"), sem("xh_done")
        ph_ready, ph_hi_done, ph_done = sem("ph_ready"), sem("ph_hi_done"), sem("ph_done")
        r_ready, r_done, rc_done, rcT_ready, rcT_hi_done, rcT_done = (
            [sem(f"{name}{g}") for g in range(G)]
            for name in ("r_ready", "r_done", "rc_done", "rcT_ready", "rcT_hi_done", "rcT_done"))
        yp_ready, yp_hi_done, yp_done = sem("yp_ready"), sem("yp_hi_done"), sem("yp_done")
        conv_ready, x2_done = sem("conv_ready"), sem("x2_done")

        h2T_ready, h2T_hi_done, h2T_done = sem("h2T_ready"), sem("h2T_hi_done"), sem("h2T_done")
        qkv_ready, qkv_copied, k_done = sem("qkv_ready"), sem("qkv_copied"), sem("k_done")
        ak_ready, w_done = sem("ak_ready"), sem("w_done")
        wrow_ready, w_nmax_done, w_exp_done = sem("wrow_ready"), sem("w_nmax_done"), sem("w_exp_done")
        w_inv_done, w_soft_done, x3_done = sem("w_inv_done"), sem("w_soft_done"), sem("x3_done")

        h3T_ready, h3T_hi_done, h3T_done = sem("h3T_ready"), sem("h3T_hi_done"), sem("h3T_done")
        zb_ready, zb_hi_done, zb_done = sem("zb_ready"), sem("zb_hi_done"), sem("zb_done")
        out_ready, x4_relu_done, x4_done = sem("out_ready"), sem("x4_relu_done"), sem("x4_done")

        SPLITS = [(t_w1[:], w1_hi[:], w1_lo[:]),
                  (t_wqk[:], wqkv_hi[:, :, :2 * ATT], wqkv_lo[:, :, :2 * ATT]),
                  (t_wv, wqkv_hi[:, :, 2 * ATT:], wqkv_lo[:, :, 2 * ATT:]),
                  (t_w3, w3_hi[:], w3_lo[:]), (wk_f[:], wk_hi[:], wk_lo[:]),
                  (t_w2g, w2_hi[:], w2_lo[:])]
        TURNS = []
        for c in range(KD):
            TURNS += [(c, h, n_w1[:, h, c * N:(c + 1) * N]) for h in range(KH)]
        for c in range(KH):
            TURNS += [(2 + c // 2, 2 * (c % 2) + o, n_w2[:, o, c * N:(c + 1) * N]) for o in range(KD)]
        for c in range(2 * KD):
            TURNS += [(4 + c // 2, 2 * (c % 2) + o, n_w3[:, o, c * N:(c + 1) * N]) for o in range(KD)]
        for c in range(KD):
            TURNS += [(6, 2 * c + o, n_wv2[:, o, c * N:(c + 1) * N]) for o in range(KD)]
        for c in range(KD):
            TURNS += [(7, c, n_wqk[:, c * N:(c + 1) * N])]
        TURNED = [(t_w1[:, 0, :], whole(0)), (t_w1[:, 1, :], whole(1)),
                  (t_w2[:, 0:2, :], wide(2)), (t_w2[:, 2:4, :], wide(3)),
                  (t_w3[:, 0:2, :], wide(4)), (t_w3[:, 2:4, :], wide(5)),
                  (t_wv, wide(6)), (t_wqk[:], halves(7))]
        LOADS = 11 + HOPS
        BIAS_LOADS = 4

        class Step:

            def __init__(self, i, u, counts=None, turns=None):
                self.i, self.u, self.counts, self.turns = i, u, counts, turns

            def on(self, lag):
                return self.counts is not None or 0 <= self.i - lag < PAIRS

            def past(self, lag):
                return self.counts is not None or self.i - lag >= 0

            def n(self, lag):
                if self.counts is None:
                    return min(self.i - lag + 1, PAIRS)
                return self.counts[self.u - lag + 1]

            def loads(self, lag):
                if self.counts is None:
                    return 32 * ((self.i - lag) // UNROLL + 1)
                return self.turns[(self.u - lag) // UNROLL]

            def slot(self, lag, slots):
                return (self.u - lag) % slots

        FIRST_STEP, LAST_STEP = -3, PAIRS + 2

        def steps(engine, step):
            for i in range(FIRST_STEP, UNROLL):
                step(Step(i, i % UNROLL))
            with engine.Fori(1, PAIRS // UNROLL - 1) as turn:
                counts = {c: engine.snap(turn * UNROLL + c) for c in range(-3, UNROLL + 4)}
                turns = [engine.snap((turn + 1) * 32), engine.snap((turn + 2) * 32)]
                for u in range(UNROLL):
                    step(Step(turn * UNROLL + u, u, counts, turns))
            for i in range(PAIRS - UNROLL, LAST_STEP + 1):
                step(Step(i, i % UNROLL))

        block = ctx.enter_context(nc.Block())

        @block.sync
        def _(sp):
            def load(dst, src, **more):
                sp.dma_start(dst, src, **more).then_inc(loaded, 16)

            def load_pair(slot, pair):
                sp.dma_start(a_in[:, slot], adj_pairs[pair]).then_inc(pair_loaded[slot], 16)
                sp.dma_start(x_in[:, slot], x_pairs[pair]).then_inc(pair_loaded[slot], 16)

            load(n_w1[:], l1_w1.rearrange("(c p) d -> p c d", p=N))
            load(n_w2[:], l1_w2.rearrange("(c p) d -> p c d", p=N))
            load(n_w3[:], l3_w.rearrange("(c p) d -> p c d", p=N))
            load(n_wv2[:], l2_wv.rearrange("(c p) d -> p c d", p=N))
            load(n_wqk[:], l2_wqk)
            load(gamma_t[:], l1_gamma.rearrange("(c p) -> p c", p=N), allow_slow_non_contiguous=True)
            load(beta_t[:], l1_beta.rearrange("(c p) -> p c", p=N), allow_slow_non_contiguous=True)
            load(n_wv0[:], l0_wv.rearrange("(c p) d -> p c d", p=N))
            load(aw_rows[:], l0_aw.rearrange("(h d) o -> (o h) d", h=2).partition_broadcast(N))
            load(bv_rows[:], l0_bv.partition_broadcast(N))
            load(ab_rows[:], l0_ab.partition_broadcast(N))
            for k in range(HOPS):
                load(wk_f[:, :, k * D:(k + 1) * D], l0_wk[k].rearrange("(c p) d -> p c d", p=N))
            sp.dma_start(b2_rows[:], l1_b2.partition_broadcast(N)).then_inc(bias_in, 16)
            sp.wait_ge(zeroed, 3)
            for row in (0, 32):
                sp.dma_start(bias_f[row:row + HOPS, BK], l0_bk).then_inc(bias_in, 16)
                sp.dma_start(bias_f[row:row + 1, B1], l1_b1.unsqueeze(0)).then_inc(bias_in, 16)
            for pair in range(UNROLL):
                load_pair(pair, pair)

            def step(s):
                if s.on(-UNROLL) and s.past(0):
                    sp.wait_ge(x1_done, s.n(0))
                    load_pair(s.slot(-UNROLL, UNROLL), s.i + UNROLL)
                if s.on(3):
                    sp.wait_ge(x4_done, s.n(3))
                    sp.dma_start(out_pairs[s.i - 3], x4[:]).then_inc(stored, 16)

            steps(sp, step)
            sp.wait_ge(stored, 16 * PAIRS)

        @block.tensor
        def _(pe):
            def product(dst, terms, bias=None):
                first = True
                if bias is not None:
                    pe.matmul(dst, ones_r[:], bias_r[:, bias], start=True, stop=False)
                    first = False
                for n, (lh, ll, rh, rl) in enumerate(terms):
                    pe.matmul(dst, lh, rh, start=first, stop=False)
                    pe.matmul(dst, lh, rl, start=False, stop=False)
                    last = pe.matmul(dst, ll, rh, start=False, stop=n == len(terms) - 1)
                    first = False
                return last

            pe.wait_ge(consts, 6)
            pe.wait_ge(loaded, 16 * LOADS)
            for b, n, block_in in TURNS:
                last = pe.transpose(psum[:, b, n * N:(n + 1) * N], block_in, ident[:])
            last.then_inc(turned, 1)
            pe.wait_ge(turned_sb, len(TURNED))
            for c in range(KH):
                last = pe.matmul(psum[:, 0, 0:D], beta_t[:, c:c + 1].broadcast_to([N, N]),
                                 t_w2[:, c, :], start=c == 0, stop=c == KH - 1)
            last.then_inc(bw_ready, 1)
            pe.wait_ge(weights_ready, 1)

            def blocks(dst, src):
                for n in range(src.shape[1]):
                    last = pe.transpose(dst[:, n * N:(n + 1) * N], src[:, n], ident[:])
                return last

            def of_pair(t):
                return t[:].rearrange("p g (c n) -> p (g c) n", n=N)

            def times(hT, g, wt, cols=slice(None), first=0):
                return [(hT[0][:, g * KD + c, :], hT[1][:, g * KD + c, :],
                         wt[0][:, first + c, cols], wt[1][:, first + c, cols]) for c in range(KD)]

            h0T, h2T, h3T, ph = (h0T_hi, h0T_lo), (h2T_hi, h2T_lo), (h3T_hi, h3T_lo), (ph_hi, ph_lo)
            wk, w1, wqkv, w3 = (wk_hi, wk_lo), (w1_hi, w1_lo), (wqkv_hi, wqkv_lo), (w3_hi, w3_lo)

            def turn_adj(s, k):
                if s.on(k):
                    pe.wait_ge(a_mean_done, s.n(k))
                    for g in range(G):
                        pe.transpose(aT_ps[:, g], a_in[:, s.slot(k, UNROLL), g], ident[:])
                    for g in range(G):
                        last = pe.transpose(amT_ps[:, g], a_mean[:, g], ident[:])
                    last.then_inc(aT_ready, 1)

            def gram(s, k):
                if s.on(k):
                    pe.wait_ge(edge_w_done, s.n(k))
                    pe.wait_ge(binc_done, s.n(k))
                    for g in range(G):
                        pe.matmul(gram_ps[:, g], inc_t[:, g], binc_hi[:, g], start=True, stop=False)
                        last = pe.matmul(gram_ps[:, g], inc_t[:, g], binc_lo[:, g],
                                         start=False, stop=True)
                    last.then_inc(gram_ready, 1)

            def turn_pt(s, k):
                if s.on(k):
                    pe.wait_ge(prop_done, s.n(k))
                    pe.wait_ge(trans_done, s.n(k))
                    for g in range(G):
                        pe.transpose(pT_ps[:, g], prop[:, g], ident[:])
                    for g in range(G):
                        last = pe.transpose(tT_ps[:, g], trans[:, g], ident[:])
                    last.then_inc(ptT_ready, 1)

            def turn_h0(s, k):
                if s.on(k):
                    pe.wait_ge(normed_done[0], s.n(k))
                    if s.past(2):
                        pe.wait_ge(w_exp_done, s.n(2))
                    blocks(h0T_ps, of_pair(normed[0])).then_inc(h0T_ready, 1)

            def y2(s, k, g):
                if s.on(k):
                    pe.wait_ge(h0T_done, s.n(k))
                    last = product(psum[:, 1 + g, 0:D + 2], times(h0T, g, wk, slice(2 * D, 3 * D + 2)))
                    if g == G - 1:
                        last.then_inc(y2_ready, 1)

            def score_rows(s, k):
                if s.on(k):
                    pe.wait_ge(s_done, s.n(k))
                    for g in range(G):
                        last = pe.transpose(e_ps[:, g], s_sb[:, g, 0:1].broadcast_to([N, N]), ident[:])
                    last.then_inc(e_ready, 1)

            def y1(s, k, g):
                if s.on(k):
                    pe.wait_ge(ptT_done, s.n(k))
                    pe.wait_ge(y2_done, s.n(k))
                    t2 = s.slot(k, 2)
                    last = product(y1_ps[:, g], times(h0T, g, wk, slice(D, 2 * D))
                                   + [(ptT_hi[:, t2, 1, g], ptT_lo[:, t2, 1, g], y2_hi[:, g], y2_lo[:, g])])
                    if g == G - 1:
                        last.then_inc(y1_ready, 1)

            def y0(s, k, g):
                if s.on(k):
                    pe.wait_ge(y1_done, s.n(k))
                    t2 = s.slot(k, 2)
                    last = product(y0_ps[:, g], times(h0T, g, wk, slice(0, D))
                                   + [(ptT_hi[:, t2, 1, g], ptT_lo[:, t2, 1, g], y1_hi[:, g], y1_lo[:, g])],
                                   BK)
                    if g == G - 1:
                        last.then_inc(y0_ready, 1)

            def propagate(s, k, g):
                if s.on(k):
                    pe.wait_ge(ptT_done, s.n(k))
                    pe.wait_ge(h1_hi_done, s.n(k))
                    pe.wait_ge(h1_lo_done, s.n(k))
                    if s.past(-1):
                        pe.wait_ge(y2_done, s.n(-1))
                    p2 = s.slot(k, 2)
                    for c in range(KD):
                        n = g * KD + c
                        cols = slice(c * N, (c + 1) * N)
                        last = product(ph_ps[:, n * N:(n + 1) * N],
                                       [(h1_hi[:, g, cols], h1_lo[:, g, cols],
                                         ptT_hi[:, p2, 0, g], ptT_lo[:, p2, 0, g])])
                    if g == G - 1:
                        last.then_inc(ph_ready, 1)

            def conv1(s, k, g):
                if s.on(k):
                    pe.wait_ge(ph_done, s.n(k))
                    product(r_ps[g], times(ph, g, w1), B1).then_inc(r_ready[g], 1)

            def turn_rc(s, k, g):
                if s.on(k):
                    pe.wait_ge(rc_done[g], s.n(k))
                    if g == 1 and s.past(-1):
                        pe.wait_ge(h0T_done, s.n(-1))
                    blocks(rcT_ps[g], rc[:, g].rearrange("p (c n) -> p c n", n=N))\
                        .then_inc(rcT_ready[g], 1)

            def conv2(s, k, g):
                if s.on(k):
                    pe.wait_ge(rcT_done[g], s.n(k))
                    last = product(yp_ps[:, g], [(rcT_hi[:, g, c], rcT_lo[:, g, c],
                                                  w2_hi[:, c], w2_lo[:, c]) for c in range(KH)], BW)
                    if g == G - 1:
                        last.then_inc(yp_ready, 1)

            def propagate2(s, k, g):
                if s.on(k):
                    pe.wait_ge(yp_done, s.n(k))
                    p2 = s.slot(k, 2)
                    last = product(conv_ps[:, g], [(ptT_hi[:, p2, 0, g], ptT_lo[:, p2, 0, g],
                                                    yp_hi[:, g], yp_lo[:, g])])
                    if g == G - 1:
                        last.then_inc(conv_ready, 1)

            def turn_h2(s, k):
                if s.on(k):
                    pe.wait_ge(normed_done[2], s.n(k))
                    if s.past(1):
                        pe.wait_ge(r_done[0], s.n(1))
                    blocks(h2T_ps, of_pair(normed[2])).then_inc(h2T_ready, 1)

            def qkv(s, k, g):
                if s.on(k):
                    pe.wait_ge(h2T_done, s.n(k))
                    last = product(qkv_ps[:, g], times(h2T, g, wqkv))
                    if g == G - 1:
                        last.then_inc(qkv_ready, 1)

            def mean_k(s, k, g):
                if s.on(k):
                    pe.wait_ge(k_done, s.n(k))
                    a4 = s.slot(k, UNROLL)
                    last = product(ak_ps[:, g], [(amT_hi[:, a4, g], amT_lo[:, a4, g],
                                                  k_hi[:, g], k_lo[:, g])])
                    if g == G - 1:
                        last.then_inc(ak_ready, 1)

            def weight_rows(s, k):
                if s.on(k):
                    pe.wait_ge(w_done, s.n(k))
                    for g in range(G):
                        last = pe.transpose(wrow_ps[:, g], w[:, g:g + 1].broadcast_to([N, N]), ident[:])
                    last.then_inc(wrow_ready, 1)

            def turn_h3(s, k):
                if s.on(k):
                    pe.wait_ge(normed_done[3], s.n(k))
                    blocks(h3T_ps, of_pair(normed[3])).then_inc(h3T_ready, 1)

            def zb(s, k, g):
                if s.on(k):
                    pe.wait_ge(h3T_done, s.n(k))
                    last = product(zb_ps[:, g], times(h3T, g, w3, first=KD))
                    if g == G - 1:
                        last.then_inc(zb_ready, 1)

            def output(s, k, g):
                if s.on(k):
                    pe.wait_ge(zb_done, s.n(k))
                    a4 = s.slot(k, UNROLL)
                    last = product(out_ps[:, g], times(h3T, g, w3)
                                   + [(amT_hi[:, a4, g], amT_lo[:, a4, g], zb_hi[:, g], zb_lo[:, g])])
                    if g == G - 1:
                        last.then_inc(out_ready, 1)

            def step(s):
                conv1(s, 1, 0)
                turn_pt(s, 0)
                conv1(s, 1, 1)
                turn_h3(s, 3)
                y1(s, 0, 0)
                turn_adj(s, -1)
                y1(s, 0, 1)
                zb(s, 3, 0)
                turn_h2(s, 2)
                zb(s, 3, 1)
                y0(s, 0, 0)
                qkv(s, 2, 0)
                y0(s, 0, 1)
                qkv(s, 2, 1)
                turn_rc(s, 1, 0)
                output(s, 3, 0)
                turn_rc(s, 1, 1)
                y2(s, -1, 0)
                mean_k(s, 2, 0)
                y2(s, -1, 1)
                mean_k(s, 2, 1)
                output(s, 3, 1)
                weight_rows(s, 2)
                conv2(s, 1, 0)
                score_rows(s, -1)
                conv2(s, 1, 1)
                propagate(s, 0, 0)
                propagate(s, 0, 1)
                turn_h0(s, -2)
                propagate2(s, 1, 0)
                gram(s, -1)
                propagate2(s, 1, 1)

            steps(pe, step)

        @block.scalar
        def _(act):
            def copy(dst, src, func=ACT.Copy):
                return nc.scalar.activation(dst, src, func)

            def joined(t):
                return t[:].rearrange("p n j -> p (n j)")

            act.wait_ge(turned, 1)
            for dst, src in TURNED:
                copy(dst, src).then_inc(turned_sb, 1)
            act.wait_ge(bias_in, 16 * (BIAS_LOADS + 1))
            copy(bias_r[:], bias_f[:]).then_inc(hi_ready, 1)
            act.wait_ge(turned_sb, len(TURNED))
            act.wait_ge(u_ready, 1)
            act.wait_ge(w2_scaled, 1)
            for src, hi, _ in SPLITS:
                copy(hi, src).then_inc(hi_ready, 1)

            def amT_part(s, k):
                if s.on(k):
                    act.wait_ge(aT_ready, s.n(k))
                    if s.past(3):
                        act.wait_ge(out_ready, s.n(3))
                    copy(amT_hi[:, s.slot(k, UNROLL)], amT_ps).then_inc(amT_hi_done, 1)

            def propagation(s, k):
                if s.on(k):
                    act.wait_ge(node_inv_done, s.n(k))
                    for g in range(G):
                        last = nc.scalar.activation(prop[:, g], gram_ps[:, g, 0:N], ACT.Copy,
                                                    scale=node_inv[:, g])
                    last.then_inc(prop_done, 1)

            def ptT_part(s, k):
                if s.on(k):
                    act.wait_ge(ptT_ready, s.n(k))
                    copy(ptT_hi[:, s.slot(k, 2)].rearrange("p k g n -> p (k g n)"), ptT_ps)\
                        .then_inc(ptT_hi_done, 1)

            def h0T_part(s, k):
                if s.on(k):
                    act.wait_ge(h0T_ready, s.n(k))
                    if s.past(0):
                        act.wait_ge(y0_ready, s.n(0))
                    copy(joined(h0T_hi), h0T_ps, ACT.Relu).then_inc(h0T_hi_done, 1)

            def y2_part(s, k):
                if s.on(k):
                    act.wait_ge(y2_ready, s.n(k))
                    copy(y2_hi[:], y2_ps).then_inc(y2_hi_done, 1)

            def score_sum(s, k):
                if s.on(k):
                    act.wait_ge(e_ready, s.n(k))
                    for g in range(G):
                        last = nc.scalar.activation(z[:, g], e_ps[:, g], ACT.Identity,
                                                    bias=s_sb[:, g, 1:2])
                    last.then_inc(z_done, 1)

            def score_exp(s, k):
                if s.on(k):
                    act.wait_ge(leaky_done, s.n(k))
                    copy(z_exp[:], z_leaky[:], ACT.Exp).then_inc(exp_done, 1)

            def y1_part(s, k):
                if s.on(k):
                    act.wait_ge(y1_ready, s.n(k))
                    copy(y1_hi[:], y1_ps).then_inc(y1_hi_done, 1)

            def h1_relu(s, k):
                if s.on(k):
                    act.wait_ge(normed_done[1], s.n(k))
                    copy(h1[:], normed[1][:], ACT.Relu).then_inc(h1_done, 1)

            def h1_part(s, k):
                if s.on(k):
                    copy(h1_hi[:], normed[1][:], ACT.Relu).then_inc(h1_hi_done, 1)

            def ph_part(s, k):
                if s.on(k):
                    act.wait_ge(ph_ready, s.n(k))
                    copy(joined(ph_hi), ph_ps).then_inc(ph_hi_done, 1)

            def r_relu(s, k, g):
                if s.on(k):
                    act.wait_ge(r_ready[g], s.n(k))
                    copy(r[:, g], r_ps[g], ACT.Relu).then_inc(r_done[g], 1)

            def rcT_part(s, k, g):
                if s.on(k):
                    act.wait_ge(rcT_ready[g], s.n(k))
                    copy(rcT_hi[:, g].rearrange("p c n -> p (c n)"), rcT_ps[g])\
                        .then_inc(rcT_hi_done[g], 1)

            def yp_part(s, k):
                if s.on(k):
                    act.wait_ge(yp_ready, s.n(k))
                    copy(yp_hi[:], yp_ps).then_inc(yp_hi_done, 1)

            def h2T_part(s, k):
                if s.on(k):
                    act.wait_ge(h2T_ready, s.n(k))
                    copy(joined(h2T_hi), h2T_ps, ACT.Relu).then_inc(h2T_hi_done, 1)

            def qkv_part(s, k):
                if s.on(k):
                    act.wait_ge(qkv_ready, s.n(k))
                    copy(k_hi[:], qkv_ps[:, :, ATT:2 * ATT])
                    copy(q_sb[:], qkv_ps[:, :, :ATT])
                    copy(v_sb[:, s.slot(k, 2)], qkv_ps[:, :, 2 * ATT:]).then_inc(qkv_copied, 1)

            def weight_exp(s, k):
                if s.on(k):
                    act.wait_ge(w_nmax_done, s.n(k))
                    for g in range(G):
                        nc.scalar.activation(w_junk[:, g], wrow_ps[:, g], ACT.Exp,
                                             bias=w_nmax[:, g:g + 1], accum_out=w_sum[:, g:g + 1])
                    for g in range(G):
                        last = nc.scalar.activation(w_exp[:, g:g + 1], w[:, g:g + 1], ACT.Exp,
                                                    bias=w_nmax[:, g:g + 1])
                    last.then_inc(w_exp_done, 1)

            def h3T_part(s, k):
                if s.on(k):
                    act.wait_ge(h3T_ready, s.n(k))
                    copy(joined(h3T_hi), h3T_ps, ACT.Relu).then_inc(h3T_hi_done, 1)

            def zb_part(s, k):
                if s.on(k):
                    act.wait_ge(zb_ready, s.n(k))
                    copy(zb_hi[:], zb_ps).then_inc(zb_hi_done, 1)

            def out_relu(s, k):
                if s.on(k):
                    act.wait_ge(out_ready, s.n(k))
                    copy(x4_relu[:], out_ps, ACT.Relu).then_inc(x4_relu_done, 1)

            def step(s):
                propagation(s, 0)
                ptT_part(s, 0)
                h3T_part(s, 3)
                r_relu(s, 1, 0)
                r_relu(s, 1, 1)
                y1_part(s, 0)
                h2T_part(s, 2)
                zb_part(s, 3)
                h0T_part(s, -1)
                qkv_part(s, 2)
                rcT_part(s, 1, 0)
                rcT_part(s, 1, 1)
                h1_relu(s, 0)
                y2_part(s, -1)
                h1_part(s, 0)
                amT_part(s, -1)
                out_relu(s, 3)
                weight_exp(s, 2)
                score_sum(s, -1)
                score_exp(s, -1)
                yp_part(s, 1)
                ph_part(s, 0)

            steps(act, step)

        @block.vector
        def _(dve):
            def rest(dst, src, hi):
                return dve.tensor_tensor(dst, src, hi.bitcast(F32), ALU.subtract)

            def relu_rest(dst, src, hi):
                return dve.scalar_tensor_tensor(out=dst, in0=src, scalar=0.0, in1=hi.bitcast(F32),
                                                op0=ALU.max, op1=ALU.subtract)

            def joined(t):
                return t[:].rearrange("p n j -> p (n j)")

            dve.wait_ge(loaded, 16 * LOADS)
            n = 0
            for c in range(KD):
                for h in range(2):
                    n += 1
                    dve.scalar_tensor_tensor(out=junk[:], in0=n_wv0[:, c], scalar=1.0,
                                             in1=aw_rows[:, h], op0=ALU.mult, op1=ALU.mult,
                                             accum_out=wk_f[:, c, HOPS * D + h:HOPS * D + h + 1])\
                       .then_inc(kappa_ready, 1)
                    dve.wait_ge(kappa_ready, n)
            for h in range(2):
                n += 1
                dve.scalar_tensor_tensor(out=junk[:], in0=bv_rows[:], scalar=1.0, in1=aw_rows[:, h],
                                         op0=ALU.mult, op1=ALU.mult, accum_out=kappa[:, h:h + 1])\
                   .then_inc(kappa_ready, 1)
                dve.wait_ge(kappa_ready, n)
            dve.tensor_tensor(kappa1[:], kappa[:, 0:1], kappa[:, 1:2], ALU.add)\
               .then_inc(kappa_ready, 1)
            dve.wait_ge(kappa_ready, n + 1)
            dve.tensor_scalar(s_const[:], kappa1[:], ab_rows[:, 0:1], 0.5, ALU.add, ALU.mult)\
               .then_inc(u_ready, 1)
            dve.wait_ge(turned_sb, 4)
            for c in range(KH):
                last = dve.tensor_scalar(t_w2g[:, c], t_w2[:, c], gamma_t[:, c:c + 1], None,
                                         ALU.mult)
            last.then_inc(w2_scaled, 1)
            dve.wait_ge(hi_ready, 1)
            rest(bias_r[32:64, 0:D + HID], bias_f[32:64, 0:D + HID], bias_r[32:64, 0:D + HID])
            dve.wait_ge(bw_ready, 1)
            dve.tensor_copy(bias_r[0:1, BW], psum[0:1, 0, 0:D])
            dve.tensor_copy(bw_hi[32:33, :], psum[32:33, 0, 0:D]).then_inc(bw_rows, 1)
            dve.wait_ge(bw_rows, 1)
            rest(bias_r[32:33, BW], psum[32:33, 0, 0:D], bw_hi[32:33, :])
            dve.wait_ge(u_ready, 1)
            dve.wait_ge(w2_scaled, 1)
            for n, (src, hi, lo) in enumerate(SPLITS):
                dve.wait_ge(hi_ready, n + 2)
                last = rest(lo, src, hi)
            last.then_inc(weights_ready, 1)

            def norm_stats(layer, src, count):
                for g in range(G):
                    last = dve.bn_stats(stats[layer][:, g], src[:, g])
                last.then_inc(stats_done[layer], 1)
                dve.wait_ge(stats_done[layer], count)
                dve.memset(held[:], 0.0)
                for g in range(G):
                    last = dve.bn_aggr(moments[layer][:, g], stats[layer][:, g])
                last.then_inc(moments_done[layer], 1)

            def norm(layer, src, count):
                dve.wait_ge(rstd_done[layer], count)
                for g in range(G):
                    last = dve.tensor_scalar(normed[layer][:, g], src[:, g],
                                             moments[layer][:, g, 0:1], rstd[layer][:, g:g + 1],
                                             ALU.subtract, ALU.mult)
                last.then_inc(normed_done[layer], 1)

            def stats0(s, k):
                if s.on(k):
                    x4_slot = s.slot(k, UNROLL)
                    dve.wait_ge(pair_loaded[x4_slot], s.loads(k))
                    norm_stats(0, x_in[:, x4_slot], s.n(k))

            def norm0(s, k):
                if s.on(k):
                    if s.past(k + 1):
                        dve.wait_ge(h0T_ready, s.n(k + 1))
                    norm(0, x_in[:, s.slot(k, UNROLL)], s.n(k))

            def degrees(s, k):
                if s.on(k):
                    a4 = s.slot(k, UNROLL)
                    dve.wait_ge(pair_loaded[a4], s.loads(k))
                    dve.tensor_reduce(deg[:], a_in[:, a4], AX_X, ALU.add).then_inc(deg_done, 1)
                    dve.wait_ge(deg_done, s.n(k))
                    dve.tensor_scalar(deg_max[:], deg[:], DEG_EPS, None, ALU.max)\
                       .then_inc(deg_max_done, 1)
                    dve.wait_ge(deg_max_done, s.n(k))
                    dve.reciprocal(deg_inv[:], deg_max[:]).then_inc(deg_inv_done, 1)
                    dve.tensor_scalar(w_scale[:, a4], deg_max[:], float(ATT) ** -0.5, None, ALU.mult)

            def incidence(s, k):
                if s.on(k):
                    a4 = s.slot(k, UNROLL)
                    edge_col = (slice(None), slice(None), slice(N, N + 1))
                    dve.wait_ge(amT_hi_done, s.n(k))
                    dve.tensor_scalar(inc_t[:], aT_ps, 0.0, None, ALU.not_equal)\
                       .then_inc(inc_done, 1)
                    dve.tensor_copy(binc_hi[edge_col], aT_ps[:, :, 0:1])
                    rest(amT_lo[:, a4], amT_ps, amT_hi[:, a4]).then_inc(amT_done, 1)
                    dve.wait_ge(inc_done, s.n(k))
                    dve.tensor_reduce(edge_cnt[:], inc_t[:].bitcast(F32), AX_X, ALU.add)\
                       .then_inc(edge_cnt_done, 1)
                    dve.wait_ge(amT_done, s.n(k))
                    rest(binc_lo[edge_col], aT_ps[:, :, 0:1], binc_hi[edge_col])\
                        .then_inc(edge_w_done, 1)

            def edge_sizes(s, k):
                if s.on(k):
                    dve.wait_ge(edge_cnt_done, s.n(k))
                    dve.tensor_scalar(edge_cnt1[:], edge_cnt[:], 1.0, None, ALU.max)\
                       .then_inc(edge_cnt1_done, 1)
                    dve.wait_ge(edge_cnt1_done, s.n(k))
                    dve.reciprocal(edge_inv[:], edge_cnt1[:]).then_inc(edge_inv_done, 1)
                    dve.wait_ge(edge_inv_done, s.n(k))
                    dve.tensor_copy(einv_hi[:], edge_inv[:]).then_inc(einv_hi_done, 1)
                    dve.wait_ge(einv_hi_done, s.n(k))
                    rest(einv_lo[:], edge_inv[:], einv_hi[:]).then_inc(einv_done, 1)

            def node_sizes(s, k):
                if s.on(k):
                    dve.wait_ge(gram_ready, s.n(k))
                    dve.tensor_scalar(node_w1[:], gram_ps[:, :, N:N + 1], TINY, None, ALU.max)\
                       .then_inc(node_w1_done, 1)
                    dve.wait_ge(node_w1_done, s.n(k))
                    dve.reciprocal(node_w2[:], node_w1[:]).then_inc(node_w2_done, 1)
                    dve.wait_ge(node_w2_done, s.n(k))
                    dve.scalar_tensor_tensor(out=node_inv[:], in0=gram_ps[:, :, N:N + 1], scalar=0.0,
                                             in1=node_w2[:], op0=ALU.is_gt, op1=ALU.mult)\
                       .then_inc(node_inv_done, 1)

            def ptT_rest(s, k):
                if s.on(k):
                    t2 = s.slot(k, 2)
                    dve.wait_ge(ptT_hi_done, s.n(k))
                    rest(ptT_lo[:, t2].rearrange("p k g n -> p (k g n)"), ptT_ps,
                         ptT_hi[:, t2].rearrange("p k g n -> p (k g n)")).then_inc(ptT_done, 1)

            def h0T_rest(s, k):
                if s.on(k):
                    dve.wait_ge(h0T_hi_done, s.n(k))
                    relu_rest(joined(h0T_lo), h0T_ps, joined(h0T_hi)).then_inc(h0T_done, 1)

            def scores(s, k):
                if s.on(k):
                    dve.wait_ge(y2_hi_done, s.n(k))
                    dve.tensor_scalar(s_sb[:], s_ps, s_const[:, 0:1], None, ALU.add)\
                       .then_inc(s_done, 1)

            def y2_rest(s, k):
                if s.on(k):
                    rest(y2_lo[:], y2_ps, y2_hi[:]).then_inc(y2_done, 1)

            def leaky(s, k):
                if s.on(k):
                    dve.wait_ge(z_done, s.n(k))
                    dve.scalar_tensor_tensor(out=z_leaky[:], in0=z[:], scalar=SLOPE, in1=z[:],
                                             op0=ALU.mult, op1=ALU.max).then_inc(leaky_done, 1)

            def alphas(s, k):
                if s.on(k):
                    dve.wait_ge(exp_done, s.n(k))
                    for g in range(G):
                        last = dve.scalar_tensor_tensor(out=alpha[:, g], in0=z_exp[:, g], scalar=1.0,
                                                        in1=a_in[:, s.slot(k, UNROLL), g],
                                                        op0=ALU.mult, op1=ALU.mult,
                                                        accum_out=row_sum[:, g:g + 1])
                    last.then_inc(alpha_done, 1)

            def row_sums(s, k):
                if s.on(k):
                    dve.wait_ge(alpha_done, s.n(k))
                    dve.tensor_scalar(row_sum1[:], row_sum[:], ROW_EPS, None, ALU.add)\
                       .then_inc(row_sum_done, 1)
                    dve.wait_ge(row_sum_done, s.n(k))
                    dve.reciprocal(row_inv[:], row_sum1[:]).then_inc(row_inv_done, 1)

            def y1_rest(s, k):
                if s.on(k):
                    dve.wait_ge(y1_hi_done, s.n(k))
                    rest(y1_lo[:], y1_ps, y1_hi[:]).then_inc(y1_done, 1)

            def sum1(s, k):
                if s.on(k):
                    dve.wait_ge(y0_ready, s.n(k))
                    dve.scalar_tensor_tensor(out=x1[:], in0=y0_ps, scalar=0.0,
                                             in1=x_in[:, s.slot(k, UNROLL)],
                                             op0=ALU.max, op1=ALU.add).then_inc(x1_done, 1)

            def stats1(s, k):
                if s.on(k):
                    dve.wait_ge(x1_done, s.n(k))
                    norm_stats(1, x1, s.n(k))

            def norm1(s, k):
                if s.on(k):
                    norm(1, x1, s.n(k))

            def ph_rest(s, k):
                if s.on(k):
                    dve.wait_ge(ph_hi_done, s.n(k))
                    rest(joined(ph_lo), ph_ps, joined(ph_hi)).then_inc(ph_done, 1)

            def r_stats(s, k, g):
                if s.on(k):
                    dve.wait_ge(r_done[g], s.n(k))
                    dve.bn_stats(stats[4][:, g], r[:, g]).then_inc(r_stats_done[g], 1)
                    dve.wait_ge(r_stats_done[g], s.n(k))
                    dve.memset(held[:], 0.0)
                    dve.bn_aggr(moments[4][:, g], stats[4][:, g]).then_inc(r_moments_done[g], 1)

            def r_norm(s, k, g):
                if s.on(k):
                    dve.wait_ge(r_rstd_done[g], s.n(k))
                    dve.tensor_scalar(rc[:, g], r[:, g], moments[4][:, g, 0:1], rstd[4][:, g:g + 1],
                                      ALU.subtract, ALU.mult).then_inc(rc_done[g], 1)

            def rcT_rest(s, k, g):
                if s.on(k):
                    dve.wait_ge(rcT_hi_done[g], s.n(k))
                    rest(rcT_lo[:, g].rearrange("p c n -> p (c n)"), rcT_ps[g],
                         rcT_hi[:, g].rearrange("p c n -> p (c n)")).then_inc(rcT_done[g], 1)

            def yp_rest(s, k):
                if s.on(k):
                    dve.wait_ge(yp_hi_done, s.n(k))
                    rest(yp_lo[:], yp_ps, yp_hi[:]).then_inc(yp_done, 1)

            def sum2(s, k):
                if s.on(k):
                    dve.wait_ge(conv_ready, s.n(k))
                    dve.wait_ge(xh_done, s.n(k))
                    dve.tensor_tensor(x2[:, s.slot(k, 2)], conv_ps, xh[:, s.slot(k, 2)], ALU.add)\
                       .then_inc(x2_done, 1)

            def stats2(s, k):
                if s.on(k):
                    dve.wait_ge(x2_done, s.n(k))
                    norm_stats(2, x2[:, s.slot(k, 2)], s.n(k))

            def norm2(s, k):
                if s.on(k):
                    norm(2, x2[:, s.slot(k, 2)], s.n(k))

            def h2T_rest(s, k):
                if s.on(k):
                    dve.wait_ge(h2T_hi_done, s.n(k))
                    relu_rest(joined(h2T_lo), h2T_ps, joined(h2T_hi)).then_inc(h2T_done, 1)

            def k_rest(s, k):
                if s.on(k):
                    dve.wait_ge(qkv_copied, s.n(k))
                    rest(k_lo[:], qkv_ps[:, :, ATT:2 * ATT], k_hi[:]).then_inc(k_done, 1)

            def weights(s, k):
                if s.on(k):
                    dve.wait_ge(ak_ready, s.n(k))
                    for g in range(G):
                        last = dve.scalar_tensor_tensor(out=qk_junk[:, g], in0=ak_ps[:, g],
                                                        scalar=w_scale[:, s.slot(k, UNROLL), g:g + 1],
                                                        in1=q_sb[:, g], op0=ALU.mult, op1=ALU.mult,
                                                        accum_out=w[:, g:g + 1])
                    last.then_inc(w_done, 1)

            def weight_max(s, k):
                if s.on(k):
                    dve.wait_ge(wrow_ready, s.n(k))
                    dve.tensor_reduce(w_nmax[:], wrow_ps, AX_X, ALU.max, negate=True)\
                       .then_inc(w_nmax_done, 1)

            def softmax(s, k):
                if s.on(k):
                    dve.wait_ge(w_exp_done, s.n(k))
                    dve.reciprocal(w_inv[:], w_sum[:]).then_inc(w_inv_done, 1)
                    dve.wait_ge(w_inv_done, s.n(k))
                    dve.tensor_tensor(w_soft[:], w_exp[:], w_inv[:], ALU.mult)\
                       .then_inc(w_soft_done, 1)

            def sum3(s, k):
                if s.on(k):
                    dve.wait_ge(w_soft_done, s.n(k))
                    for g in range(G):
                        last = dve.scalar_tensor_tensor(out=x3[:, s.slot(k, 2), g],
                                                        in0=v_sb[:, s.slot(k, 2), g],
                                                        scalar=w_soft[:, g:g + 1],
                                                        in1=x2[:, s.slot(k, 2), g],
                                                        op0=ALU.mult, op1=ALU.add)
                    last.then_inc(x3_done, 1)

            def stats3(s, k):
                if s.on(k):
                    dve.wait_ge(x3_done, s.n(k))
                    norm_stats(3, x3[:, s.slot(k, 2)], s.n(k))

            def norm3(s, k):
                if s.on(k):
                    norm(3, x3[:, s.slot(k, 2)], s.n(k))

            def h3T_rest(s, k):
                if s.on(k):
                    dve.wait_ge(h3T_hi_done, s.n(k))
                    relu_rest(joined(h3T_lo), h3T_ps, joined(h3T_hi)).then_inc(h3T_done, 1)

            def zb_rest(s, k):
                if s.on(k):
                    dve.wait_ge(zb_hi_done, s.n(k))
                    rest(zb_lo[:], zb_ps, zb_hi[:]).then_inc(zb_done, 1)

            def step(s):
                stats3(s, 3)
                degrees(s, -1)
                sum2(s, 2)
                norm3(s, 3)
                ptT_rest(s, 0)
                stats2(s, 2)
                h3T_rest(s, 3)
                r_stats(s, 1, 0)
                norm2(s, 2)
                y1_rest(s, 0)
                h2T_rest(s, 2)
                r_stats(s, 1, 1)
                zb_rest(s, 3)
                r_norm(s, 1, 0)
                norm0(s, -2)
                r_norm(s, 1, 1)
                sum1(s, 0)
                h0T_rest(s, -1)
                stats1(s, 0)
                k_rest(s, 2)
                stats0(s, -3)
                norm1(s, 0)
                rcT_rest(s, 1, 0)
                rcT_rest(s, 1, 1)
                weights(s, 2)
                scores(s, -1)
                y2_rest(s, -1)
                weight_max(s, 2)
                incidence(s, -1)
                softmax(s, 2)
                edge_sizes(s, -1)
                leaky(s, -1)
                sum3(s, 2)
                alphas(s, -1)
                yp_rest(s, 1)
                row_sums(s, -1)
                ph_rest(s, 0)
                node_sizes(s, -1)

            steps(dve, step)

        @block.gpsimd
        def _(pool):
            pool.memset(bias_f[:], 0.0).then_inc(zeroed, 1)
            pool.memset(binc_hi[:].bitcast(F32), 0.0).then_inc(zeroed, 1)
            pool.memset(binc_lo[:].bitcast(F32), 0.0).then_inc(zeroed, 1)
            pool.memset(ones_r[:].bitcast(F32), 1.0).then_inc(consts, 1)
            pool.memset(eps_ln[:], LN_EPS).then_inc(consts, 1)
            pool.memset(minus_half[:], -0.5).then_inc(consts, 1)
            pool.memset(ident[:], 0.0).then_inc(consts, 1)
            pool.wait_ge(consts, 4)
            pool.affine_select(out=ident[:], in_=ident[:], compare_op=ALU.not_equal, fill=1.0, base=0,
                               pattern=[[-1, N]], channel_multiplier=1).then_inc(consts, 2)
            pool.wait_ge(consts, 6)
            pool.wait_ge(zeroed, 3)
            pool.wait_ge(bias_in, 16 * (BIAS_LOADS + 1))

            def inverse_std(s, k, layer):
                if s.on(k):
                    pool.wait_ge(moments_done[layer], s.n(k))
                    pool.tensor_tensor(var_eps[layer][:], moments[layer][:, :, 1], eps_ln[:], ALU.add)\
                        .then_inc(var_done[layer], 1)
                    pool.wait_ge(var_done[layer], s.n(k))
                    pool.tensor_tensor(rstd[layer][:], var_eps[layer][:], minus_half[:], ALU.pow)\
                        .then_inc(rstd_done[layer], 1)

            def r_inverse_std(s, k, g):
                if s.on(k):
                    pool.wait_ge(r_moments_done[g], s.n(k))
                    pool.tensor_tensor(var_eps[4][:, g:g + 1], moments[4][:, g, 1:2],
                                       eps_ln[:, g:g + 1], ALU.add).then_inc(r_var_done[g], 1)
                    pool.wait_ge(r_var_done[g], s.n(k))
                    pool.tensor_tensor(rstd[4][:, g:g + 1], var_eps[4][:, g:g + 1],
                                       minus_half[:, g:g + 1], ALU.pow).then_inc(r_rstd_done[g], 1)

            def rows(v):
                return v.unsqueeze(2).broadcast_to([N, G, N])

            def mean_matrix(s, k):
                if s.on(k):
                    pool.wait_ge(deg_inv_done, s.n(k))
                    pool.tensor_tensor(a_mean[:], a_in[:, s.slot(k, UNROLL)], rows(deg_inv[:]),
                                       ALU.mult).then_inc(a_mean_done, 1)

            def scaled_incidence(s, k):
                if s.on(k):
                    pool.wait_ge(einv_done, s.n(k))
                    pool.tensor_tensor(binc_hi[:, :, 0:N], inc_t[:].bitcast(F32),
                                       rows(einv_hi[:].bitcast(F32)), ALU.mult)
                    pool.tensor_tensor(binc_lo[:, :, 0:N], inc_t[:].bitcast(F32),
                                       rows(einv_lo[:].bitcast(F32)), ALU.mult)\
                        .then_inc(binc_done, 1)

            def transition(s, k):
                if s.on(k):
                    pool.wait_ge(row_inv_done, s.n(k))
                    pool.tensor_tensor(trans[:], alpha[:], rows(row_inv[:]), ALU.mult)\
                        .then_inc(trans_done, 1)

            def h1_rest(s, k):
                if s.on(k):
                    pool.wait_ge(h1_hi_done, s.n(k))
                    pool.tensor_tensor(h1_lo[:], h1[:], h1_hi[:].bitcast(F32), ALU.subtract)\
                        .then_inc(h1_lo_done, 1)

            def residual1(s, k):
                if s.on(k):
                    pool.wait_ge(h1_done, s.n(k))
                    pool.tensor_tensor(x1b[:], x1[:], b2_rows[:].unsqueeze(1).broadcast_to([N, G, D]),
                                       ALU.add).then_inc(x1b_done, 1)
                    pool.wait_ge(x1b_done, s.n(k))
                    pool.tensor_tensor(xh[:, s.slot(k, 2)], x1b[:], h1[:], ALU.add)\
                        .then_inc(xh_done, 1)

            def sum4(s, k):
                if s.on(k):
                    pool.wait_ge(x4_relu_done, s.n(k))
                    if s.past(k + 1):
                        pool.wait_ge(stored, 16 * s.n(k + 1))
                    pool.tensor_tensor(x4[:], x4_relu[:], x3[:, s.slot(k, 2)], ALU.add)\
                        .then_inc(x4_done, 1)

            def step(s):
                transition(s, 0)
                inverse_std(s, 3, 3)
                mean_matrix(s, -1)
                inverse_std(s, 2, 2)
                r_inverse_std(s, 1, 0)
                residual1(s, 1)
                r_inverse_std(s, 1, 1)
                inverse_std(s, 0, 1)
                h1_rest(s, 0)
                sum4(s, 3)
                scaled_incidence(s, -1)
                inverse_std(s, -3, 0)

            steps(pool, step)


_INS = ['x', 'adj', 'L0_gnn_Wv', 'L0_gnn_bv', 'L0_gnn_aw', 'L0_gnn_ab', 'L0_gnn_Wk', 'L0_gnn_bk',
        'L1_gnn_W1', 'L1_gnn_b1', 'L1_gnn_gamma', 'L1_gnn_beta', 'L1_gnn_W2', 'L1_gnn_b2',
        'L2_gnn_W_qk', 'L2_gnn_W_v', 'L3_gnn_W']


def kernel(**inputs):
    import numpy as np
    import concourse.bacc as bacc
    from concourse.bass_utils import run_bass_kernel_spmd

    nc = bacc.Bacc("TRN2", target_bir_lowering=False, num_devices=1)
    arrays, args = {}, []
    for name in _INS:
        a = np.ascontiguousarray(inputs[name])
        arrays[f"in_{name}"] = a
        args.append(nc.dram_tensor(f"in_{name}", a.shape, mybir.dt.from_np(a.dtype),
                                   kind="ExternalInput").ap())
    out = nc.dram_tensor("out_x", inputs["x"].shape, F32, kind="ExternalOutput").ap()
    build_program(nc, *args, out)
    result = run_bass_kernel_spmd(nc, [arrays], core_ids=[0])
    return result.results[0]["out_x"]
```

```python
from contextlib import ExitStack

import concourse.bass as bass
from concourse import mybir

F32 = mybir.dt.float32
F32R = mybir.dt.float32r
ALU = mybir.AluOpType
ACT = mybir.ActivationFunctionType
AX_X = mybir.AxisListType.X

LN_EPS = 1e-5
ROW_EPS = 1e-12
DEG_EPS = 1e-6
SLOPE = 0.2
TINY = 1e-38
UNROLL = 4


def build_program(nc, x, adj, l0_wv, l0_bv, l0_aw, l0_ab, l0_wk, l0_bk, l1_w1, l1_b1, l1_gamma,
                  l1_beta, l1_w2, l1_b2, l2_wqk, l2_wv, l3_w, out):
    graphs, N, D = x.shape
    G = 2
    PAIRS = graphs // G
    KD = D // N
    HID = l1_w1.shape[0]
    KH = HID // N
    ATT = l2_wqk.shape[0] // 2
    HOPS = l0_wk.shape[0]
    assert N == 128 and D == 256 and HID == 512 and HOPS == 3 and ATT == 64 and PAIRS % UNROLL == 0

    x_pairs = x.rearrange("(p g) n d -> p n g d", g=G)
    adj_pairs = adj.rearrange("(p g) i j -> p i g j", g=G)
    out_pairs = out.rearrange("(p g) n d -> p n g d", g=G)

    with ExitStack() as ctx:
        def sb(name, shape, dt=F32):
            return ctx.enter_context(nc.sbuf_tensor(name, shape, dt))

        def sem(name):
            return ctx.enter_context(nc.semaphore(name))

        def split(name, shape):
            return sb(name + "_hi", shape, F32R), sb(name + "_lo", shape, F32R)

        ident = sb("ident", [N, N])
        ones_r = sb("ones_r", [N, N], F32R)
        eps_ln = sb("eps_ln", [N, G])
        minus_half = sb("minus_half", [N, G])
        hid_inv = sb("hid_inv", [N, G])
        hid_ninv = sb("hid_ninv", [N, G])
        s_const = sb("s_const", [N, 1])
        wk_hi, wk_lo = split("wk", [N, KD, HOPS * D + 2])
        w1_hi, w1_lo = split("w1", [N, KD, HID])
        w2_hi, w2_lo = split("w2", [N, KH, D])
        wqkv_hi, wqkv_lo = split("wqkv", [N, KD, 2 * ATT + D])
        w3_hi, w3_lo = split("w3", [N, 2 * KD, D])
        b2_rows = sb("b2_rows", [N, D])
        bw_all = sb("bw_all", [N, D])
        BK, B1 = slice(0, D), slice(D, D + HID)
        bias_f = sb("bias_f", [N, D + HID])
        bias_r = sb("bias_r", [N, D + HID], F32R)

        n_w2 = sb("n_w2", [N, KD, HID])
        n_wqk = sb("n_wqk", [N, D])
        n_w3 = sb("n_w3", [N, KD, 2 * D])
        bv_rows = sb("bv_rows", [N, D])
        ab_rows = sb("ab_rows", [N, 1])
        gamma_t = sb("gamma_t", [N, KH])
        beta_t = sb("beta_t", [N, KH])
        kappa = sb("kappa", [N, 2])
        kappa1 = sb("kappa1", [N, 1])
        junk = sb("junk", [N, D])
        t_wqk = sb("t_wqk", [N, KD, 2 * ATT])

        x_in = sb("x_in", [N, UNROLL, G, D])
        a_in = sb("a_in", [N, UNROLL, G, N])
        deg = sb("deg", [N, G])
        deg_max = sb("deg_max", [N, UNROLL, G])
        deg_inv = sb("deg_inv", [N, UNROLL, G])
        aT_hi, aT_lo = split("aT", [N, UNROLL, G, N])
        inc_t = sb("inc_t", [N, G, N], F32R)
        edge_cnt = sb("edge_cnt", [N, G])
        edge_cnt1 = sb("edge_cnt1", [N, G])
        edge_inv = sb("edge_inv", [N, G])
        einv_hi, einv_lo = split("einv", [N, G])
        binc_hi, binc_lo = split("binc", [N, G, N + 2])
        node_w1 = sb("node_w1", [N, G, 1])
        node_w2 = sb("node_w2", [N, G, 1])
        node_inv = sb("node_inv", [N, G, 1])
        prop = sb("prop", [N, 2, G, N + 2])
        ptT_hi, ptT_lo = split("ptT", [N, 2, 2, G, N])
        stats = [sb(f"stats{n}", [N, G, 6]) for n in range(4)]
        moments = [sb(f"moments{n}", [N, G, 2]) for n in range(4)]
        var_eps = [sb(f"var_eps{n}", [N, G]) for n in range(4)]
        rstd = [sb(f"rstd{n}", [N, G]) for n in range(4)]
        normed = [sb(f"normed{n}", [N, G, D]) for n in range(4)]
        held = sb("held", [N, 1])
        rstd_deg = sb("rstd_deg", [N, G])

        h0T_hi, h0T_lo = split("h0T", [N, G * KD, N])
        s_sb = sb("s_sb", [N, G, 2])
        y2_hi, y2_lo = split("y2", [N, G, D])
        y1_hi, y1_lo = split("y1", [N, G, D])
        z = sb("z", [N, G, N])
        z_leaky = sb("z_leaky", [N, G, N])
        z_exp = sb("z_exp", [N, G, N])
        alpha = sb("alpha", [N, G, N])
        row_sum = sb("row_sum", [N, G])
        row_sum1 = sb("row_sum1", [N, G])
        row_inv = sb("row_inv", [N, G])
        trans = sb("trans", [N, G, N])
        x1 = sb("x1", [N, G, D])

        h1 = sb("h1", [N, G, D])
        h1_hi, h1_lo = split("h1", [N, G, D])
        x1b = sb("x1b", [N, G, D])
        xbh = sb("xbh", [N, G, D])
        p_bw = sb("p_bw", [N, G, D])
        xh = sb("xh", [N, 2, G, D])
        ph_hi, ph_lo = split("ph", [N, G * KD, N])
        r = sb("r", [N, G, HID])
        r_sum = sb("r_sum", [N, G])
        r_nmean = sb("r_nmean", [N, G])
        r_dev = sb("r_dev", [N, HID])
        r_part_ss = sb("r_part_ss", [N, G, KH])
        r_half_ss = sb("r_half_ss", [N, G, 2])
        r_ss = sb("r_ss", [N, G])
        r_var = sb("r_var", [N, G])
        r_var_eps = sb("r_var_eps", [N, G])
        r_rstd = sb("r_rstd", [N, G])
        rT_hi, rT_lo = split("rT", [N, G, KH, N])
        yp_hi, yp_lo = split("yp", [N, G, D])
        x2 = sb("x2", [N, 2, G, D])

        h2T_hi, h2T_lo = split("h2T", [N, G * KD, N])
        q_sb = sb("q_sb", [N, G, ATT])
        k_parts = sb("k_parts", [N, G, 2, ATT], F32R)
        v_sb = sb("v_sb", [N, 2, G, D])
        qk_junk = sb("qk_junk", [N, G, 2, ATT])
        w = sb("w", [N, G])
        w_nmax = sb("w_nmax", [N, G])
        w_junk = sb("w_junk", [N, G, N])
        w_sum = sb("w_sum", [N, G])
        w_exp = sb("w_exp", [N, G])
        w_inv = sb("w_inv", [N, G])
        w_soft = sb("w_soft", [N, G])
        x3 = sb("x3", [N, 2, G, D])

        h3T_hi, h3T_lo = split("h3T", [N, G * KD, N])
        zb_hi, zb_lo = split("zb", [N, G, D])
        x4_relu = sb("x4_relu", [N, G, D])
        x4 = sb("x4", [N, G, D])

        n_wv0, n_wv2, aw_rows = normed[1], normed[2], normed[3]
        n_w1 = v_sb[:].rearrange("p s g d -> p (s g) d")
        t_w1 = r
        t_w2 = [t[:, c] for t in (x4, x4_relu) for c in range(KD)]
        t_w2g = xh[:].rearrange("p s g d -> p (s g) d")
        t_w3 = x2[:].rearrange("p s g d -> p (s g) d")
        t_wv = x3[:, 0]
        wk_f = sb("wk_f", [N, KD, HOPS * D + 2])

        psum = ctx.enter_context(nc.psum_tensor("psum", [N, 8, 512], F32))

        def whole(b):
            return psum[:, b, :]

        def halves(b, first=0):
            return psum[:, b, first:first + G * N].rearrange("p (g n) -> p g n", g=G)

        def wide(b):
            return psum[:, b, :].rearrange("p (g d) -> p g d", g=G)

        yp_ps, r1_ps, rT1_ps = wide(0), whole(0), whole(0)
        qkv_ps = psum[:, 0:2, 0:2 * ATT + D]
        e_ps, pT_ps, tT_ps, ptT_ps, h2T_ps = halves(1), halves(1), halves(1, G * N), whole(1), whole(1)
        ak_ps = psum[:, 2, 0:G * 2 * ATT].rearrange("p (g t a) -> p g t a", g=G, t=2)
        h0T_ps = whole(2)
        wrow_ps, r0_ps, rT0_ps, out_ps = halves(3), whole(3), whole(3), wide(3)
        aT_ps = halves(4)
        y2_ps, s_ps = psum[:, 5:7, 0:D], psum[:, 5:7, D:D + 2]
        conv_ps, h3T_ps, y0_ps = wide(5), whole(5), wide(5)
        gram_ps = psum[:, 6, 0:G * (N + 2)].rearrange("p (g n) -> p g n", g=G)
        y1_ps = wide(6)
        ph_ps, zb_ps = whole(7), wide(7)
        r_ps, rT_ps = [r0_ps, r1_ps], [rT0_ps, rT1_ps]

        zeroed = sem("zeroed")
        consts = sem("consts")
        loaded = sem("loaded")
        bias_in = sem("bias_in")
        turned = sem("turned")
        turned_sb = sem("turned_sb")
        w2_scaled = sem("w2_scaled")
        bw_ready = sem("bw_ready")
        w2_mean_ready = sem("w2_mean_ready")
        kappa_ready = sem("kappa_ready")
        u_ready = sem("u_ready")
        hi_ready = sem("hi_ready")
        w2_centred = sem("w2_centred")
        weights_ready = sem("weights_ready")

        pair_loaded = [sem(f"pair_loaded{k}") for k in range(UNROLL)]
        stored = sem("stored")
        stats_done, moments_done, var_done, rstd_done, normed_done = (
            [sem(f"{name}_done{n}") for n in range(4)]
            for name in ("stats", "moments", "var", "rstd", "normed"))
        (r_mean_done, r_squares_done, r_half_ss_done, r_ss_done, r_var_done, r_var_eps_done,
         r_rstd_done) = (
            [sem(f"{name}_done{g}") for g in range(G)]
            for name in ("r_mean", "r_squares", "r_half_ss", "r_ss", "r_var", "r_var_eps", "r_rstd"))
        deg_done, deg_max_done, deg_inv_done = sem("deg_done"), sem("deg_max_done"), sem("deg_inv_done")
        rstd_deg_done = sem("rstd_deg_done")
        aT_ready, aT_hi_done, aT_done = sem("aT_ready"), sem("aT_hi_done"), sem("aT_done")
        inc_done, edge_w_done, edge_cnt_done = sem("inc_done"), sem("edge_w_done"), sem("edge_cnt_done")
        edge_cnt1_done, edge_inv_done = sem("edge_cnt1_done"), sem("edge_inv_done")
        einv_hi_done, einv_done = sem("einv_hi_done"), sem("einv_done")
        binc_done = sem("binc_done")
        gram_ready = sem("gram_ready")
        node_w1_done, node_w2_done = sem("node_w1_done"), sem("node_w2_done")
        node_inv_done = sem("node_inv_done")
        prop_done = sem("prop_done")
        ptT_ready, ptT_hi_done, ptT_done = sem("ptT_ready"), sem("ptT_hi_done"), sem("ptT_done")

        h0T_ready, h0T_hi_done, h0T_done = sem("h0T_ready"), sem("h0T_hi_done"), sem("h0T_done")
        y2_ready, y2_hi_done, y2_done = sem("y2_ready"), sem("y2_hi_done"), sem("y2_done")
        s_done = sem("s_done")
        e_ready, z_done, leaky_done, exp_done = sem("e_ready"), sem("z_done"), sem("leaky_done"), sem("exp_done")
        alpha_done, row_sum_done, row_inv_done = sem("alpha_done"), sem("row_sum_done"), sem("row_inv_done")
        trans_done = sem("trans_done")
        y1_ready, y1_hi_done, y1_done = sem("y1_ready"), sem("y1_hi_done"), sem("y1_done")
        y0_ready, x1_done = sem("y0_ready"), sem("x1_done")

        h1_done, h1_hi_done, h1_lo_done = sem("h1_done"), sem("h1_hi_done"), sem("h1_lo_done")
        x1b_done, xbh_done, xh_done = sem("x1b_done"), sem("xbh_done"), sem("xh_done")
        ph_ready, ph_hi_done, ph_done = sem("ph_ready"), sem("ph_hi_done"), sem("ph_done")
        r_ready, r_done, rT_ready, rT_hi_done, rT_done = (
            [sem(f"{name}{g}") for g in range(G)]
            for name in ("r_ready", "r_done", "rT_ready", "rT_hi_done", "rT_done"))
        yp_ready, yp_hi_done, yp_done = sem("yp_ready"), sem("yp_hi_done"), sem("yp_done")
        conv_ready, x2_done = sem("conv_ready"), sem("x2_done")

        h2T_ready, h2T_hi_done, h2T_done = sem("h2T_ready"), sem("h2T_hi_done"), sem("h2T_done")
        qkv_ready, qkv_copied, k_done = sem("qkv_ready"), sem("qkv_copied"), sem("k_done")
        ak_ready, w_done = sem("ak_ready"), sem("w_done")
        wrow_ready, w_nmax_done, w_exp_done = sem("wrow_ready"), sem("w_nmax_done"), sem("w_exp_done")
        w_inv_done, w_soft_done, x3_done = sem("w_inv_done"), sem("w_soft_done"), sem("x3_done")

        h3T_ready, h3T_hi_done, h3T_done = sem("h3T_ready"), sem("h3T_hi_done"), sem("h3T_done")
        zb_ready, zb_hi_done, zb_done = sem("zb_ready"), sem("zb_hi_done"), sem("zb_done")
        out_ready, x4_relu_done, x4_done = sem("out_ready"), sem("x4_relu_done"), sem("x4_done")

        SPLITS = [(t_w1[:], w1_hi[:], w1_lo[:]),
                  (t_wqk[:], wqkv_hi[:, :, :2 * ATT], wqkv_lo[:, :, :2 * ATT]),
                  (t_wv, wqkv_hi[:, :, 2 * ATT:], wqkv_lo[:, :, 2 * ATT:]),
                  (t_w3, w3_hi[:], w3_lo[:]), (wk_f[:], wk_hi[:], wk_lo[:]),
                  (t_w2g, w2_hi[:], w2_lo[:])]
        TURNS = []
        for c in range(KD):
            TURNS += [(c, h, n_w1[:, h, c * N:(c + 1) * N]) for h in range(KH)]
        for c in range(KH):
            TURNS += [(2 + c // 2, 2 * (c % 2) + o, n_w2[:, o, c * N:(c + 1) * N]) for o in range(KD)]
        for c in range(2 * KD):
            TURNS += [(4 + c // 2, 2 * (c % 2) + o, n_w3[:, o, c * N:(c + 1) * N]) for o in range(KD)]
        for c in range(KD):
            TURNS += [(6, 2 * c + o, n_wv2[:, o, c * N:(c + 1) * N]) for o in range(KD)]
        for c in range(KD):
            TURNS += [(7, c, n_wqk[:, c * N:(c + 1) * N])]
        TURNED = [(t_w1[:, 0, :], whole(0)), (t_w1[:, 1, :], whole(1)),
                  (x4[:], wide(2)), (x4_relu[:], wide(3)),
                  (t_w3[:, 0:2, :], wide(4)), (t_w3[:, 2:4, :], wide(5)),
                  (t_wv, wide(6)), (t_wqk[:], halves(7))]
        LOADS = 11 + HOPS
        BIAS_LOADS = 4

        class Step:

            def __init__(self, i, u, counts=None, turns=None):
                self.i, self.u, self.counts, self.turns = i, u, counts, turns

            def on(self, lag):
                return self.counts is not None or 0 <= self.i - lag < PAIRS

            def past(self, lag):
                return self.counts is not None or self.i - lag >= 0

            def n(self, lag):
                if self.counts is None:
                    return min(self.i - lag + 1, PAIRS)
                return self.counts[self.u - lag + 1]

            def loads(self, lag):
                if self.counts is None:
                    return 32 * ((self.i - lag) // UNROLL + 1)
                return self.turns[(self.u - lag) // UNROLL]

            def slot(self, lag, slots):
                return (self.u - lag) % slots

        FIRST_STEP, LAST_STEP = -3, PAIRS + 2

        def steps(engine, step):
            for i in range(FIRST_STEP, UNROLL):
                step(Step(i, i % UNROLL))
            with engine.Fori(1, PAIRS // UNROLL - 1) as turn:
                counts = {c: engine.snap(turn * UNROLL + c) for c in range(-3, UNROLL + 4)}
                turns = [engine.snap((turn + 1) * 32), engine.snap((turn + 2) * 32)]
                for u in range(UNROLL):
                    step(Step(turn * UNROLL + u, u, counts, turns))
            for i in range(PAIRS - UNROLL, LAST_STEP + 1):
                step(Step(i, i % UNROLL))

        block = ctx.enter_context(nc.Block())

        @block.sync
        def _(sp):
            def load(dst, src, **more):
                sp.dma_start(dst, src, **more).then_inc(loaded, 16)

            def load_pair(slot, pair):
                sp.dma_start(a_in[:, slot], adj_pairs[pair]).then_inc(pair_loaded[slot], 16)
                sp.dma_start(x_in[:, slot], x_pairs[pair]).then_inc(pair_loaded[slot], 16)

            load(n_w1[:], l1_w1.rearrange("(c p) d -> p c d", p=N))
            load(n_w2[:], l1_w2.rearrange("(c p) d -> p c d", p=N))
            load(n_w3[:], l3_w.rearrange("(c p) d -> p c d", p=N))
            load(n_wv2[:], l2_wv.rearrange("(c p) d -> p c d", p=N))
            load(n_wqk[:], l2_wqk)
            load(gamma_t[:], l1_gamma.rearrange("(c p) -> p c", p=N), allow_slow_non_contiguous=True)
            load(beta_t[:], l1_beta.rearrange("(c p) -> p c", p=N), allow_slow_non_contiguous=True)
            load(n_wv0[:], l0_wv.rearrange("(c p) d -> p c d", p=N))
            load(aw_rows[:], l0_aw.rearrange("(h d) o -> (o h) d", h=2).partition_broadcast(N))
            load(bv_rows[:], l0_bv.partition_broadcast(N))
            load(ab_rows[:], l0_ab.partition_broadcast(N))
            for k in range(HOPS):
                load(wk_f[:, :, k * D:(k + 1) * D], l0_wk[k].rearrange("(c p) d -> p c d", p=N))
            sp.dma_start(b2_rows[:], l1_b2.partition_broadcast(N)).then_inc(bias_in, 16)
            sp.wait_ge(zeroed, 3)
            for row in (0, 32):
                sp.dma_start(bias_f[row:row + HOPS, BK], l0_bk).then_inc(bias_in, 16)
                sp.dma_start(bias_f[row:row + 1, B1], l1_b1.unsqueeze(0)).then_inc(bias_in, 16)
            for pair in range(UNROLL):
                load_pair(pair, pair)

            def step(s):
                if s.on(-UNROLL) and s.past(0):
                    sp.wait_ge(x1_done, s.n(0))
                    load_pair(s.slot(-UNROLL, UNROLL), s.i + UNROLL)
                if s.on(3):
                    sp.wait_ge(x4_done, s.n(3))
                    sp.dma_start(out_pairs[s.i - 3], x4[:]).then_inc(stored, 16)

            steps(sp, step)
            sp.wait_ge(stored, 16 * PAIRS)

        @block.tensor
        def _(pe):
            def product(dst, terms, bias=None):
                first = True
                if bias is not None:
                    pe.matmul(dst, ones_r[:], bias_r[:, bias], start=True, stop=False)
                    first = False
                for n, (lh, ll, rh, rl) in enumerate(terms):
                    pe.matmul(dst, lh, rh, start=first, stop=False)
                    pe.matmul(dst, lh, rl, start=False, stop=False)
                    last = pe.matmul(dst, ll, rh, start=False, stop=n == len(terms) - 1)
                    first = False
                return last

            pe.wait_ge(consts, 8)
            pe.wait_ge(loaded, 16 * LOADS)
            for b, n, block_in in TURNS:
                last = pe.transpose(psum[:, b, n * N:(n + 1) * N], block_in, ident[:])
            last.then_inc(turned, 1)
            pe.wait_ge(turned_sb, len(TURNED))
            for c in range(KH):
                last = pe.matmul(psum[:, 0, 0:D], beta_t[:, c:c + 1].broadcast_to([N, N]),
                                 t_w2[c], start=c == 0, stop=c == KH - 1)
            last.then_inc(bw_ready, 1)
            pe.wait_ge(w2_scaled, 1)
            for c in range(KH):
                last = pe.matmul(psum[:, 1, 0:D], hid_inv[:, 0:1].broadcast_to([N, N]),
                                 t_w2g[:, c, :], start=c == 0, stop=c == KH - 1)
            last.then_inc(w2_mean_ready, 1)
            pe.wait_ge(weights_ready, 1)

            def blocks(dst, src):
                for n in range(src.shape[1]):
                    last = pe.transpose(dst[:, n * N:(n + 1) * N], src[:, n], ident[:])
                return last

            def of_pair(t):
                return t[:].rearrange("p g (c n) -> p (g c) n", n=N)

            def times(hT, g, wt, cols=slice(None), first=0):
                return [(hT[0][:, g * KD + c, :], hT[1][:, g * KD + c, :],
                         wt[0][:, first + c, cols], wt[1][:, first + c, cols]) for c in range(KD)]

            h0T, h2T, h3T, ph = (h0T_hi, h0T_lo), (h2T_hi, h2T_lo), (h3T_hi, h3T_lo), (ph_hi, ph_lo)
            wk, w1, wqkv, w3 = (wk_hi, wk_lo), (w1_hi, w1_lo), (wqkv_hi, wqkv_lo), (w3_hi, w3_lo)

            def turn_adj(s, k):
                if s.on(k):
                    a4 = s.slot(k, UNROLL)
                    pe.wait_ge(pair_loaded[a4], s.loads(k))
                    for g in range(G):
                        last = pe.transpose(aT_ps[:, g], a_in[:, a4, g], ident[:])
                    last.then_inc(aT_ready, 1)

            def gram(s, k):
                if s.on(k):
                    pe.wait_ge(edge_w_done, s.n(k))
                    pe.wait_ge(binc_done, s.n(k))
                    pe.wait_ge(y2_done, s.n(k))
                    for g in range(G):
                        pe.matmul(gram_ps[:, g], inc_t[:, g], binc_hi[:, g], start=True, stop=False)
                        last = pe.matmul(gram_ps[:, g], inc_t[:, g], binc_lo[:, g],
                                         start=False, stop=True)
                    last.then_inc(gram_ready, 1)

            def turn_pt(s, k):
                if s.on(k):
                    pe.wait_ge(prop_done, s.n(k))
                    pe.wait_ge(trans_done, s.n(k))
                    for g in range(G):
                        pe.transpose(pT_ps[:, g], prop[:, s.slot(k, 2), g, 0:N], ident[:])
                    for g in range(G):
                        last = pe.transpose(tT_ps[:, g], trans[:, g], ident[:])
                    last.then_inc(ptT_ready, 1)

            def turn_h0(s, k):
                if s.on(k):
                    pe.wait_ge(normed_done[0], s.n(k))
                    blocks(h0T_ps, of_pair(normed[0])).then_inc(h0T_ready, 1)

            def y2(s, k, g):
                if s.on(k):
                    pe.wait_ge(h0T_done, s.n(k))
                    last = product(psum[:, 5 + g, 0:D + 2], times(h0T, g, wk, slice(2 * D, 3 * D + 2)))
                    if g == G - 1:
                        last.then_inc(y2_ready, 1)

            def score_rows(s, k):
                if s.on(k):
                    pe.wait_ge(s_done, s.n(k))
                    for g in range(G):
                        last = pe.transpose(e_ps[:, g], s_sb[:, g, 0:1].broadcast_to([N, N]), ident[:])
                    last.then_inc(e_ready, 1)

            def y1(s, k, g):
                if s.on(k):
                    pe.wait_ge(ptT_done, s.n(k))
                    pe.wait_ge(y2_done, s.n(k))
                    t2 = s.slot(k, 2)
                    last = product(y1_ps[:, g], times(h0T, g, wk, slice(D, 2 * D))
                                   + [(ptT_hi[:, t2, 1, g], ptT_lo[:, t2, 1, g], y2_hi[:, g], y2_lo[:, g])])
                    if g == G - 1:
                        last.then_inc(y1_ready, 1)

            def y0(s, k, g):
                if s.on(k):
                    pe.wait_ge(y1_done, s.n(k))
                    t2 = s.slot(k, 2)
                    last = product(y0_ps[:, g], times(h0T, g, wk, slice(0, D))
                                   + [(ptT_hi[:, t2, 1, g], ptT_lo[:, t2, 1, g], y1_hi[:, g], y1_lo[:, g])],
                                   BK)
                    if g == G - 1:
                        last.then_inc(y0_ready, 1)

            def propagate(s, k, g):
                if s.on(k):
                    pe.wait_ge(ptT_done, s.n(k))
                    pe.wait_ge(h1_hi_done, s.n(k))
                    pe.wait_ge(h1_lo_done, s.n(k))
                    p2 = s.slot(k, 2)
                    for c in range(KD):
                        n = g * KD + c
                        cols = slice(c * N, (c + 1) * N)
                        last = product(ph_ps[:, n * N:(n + 1) * N],
                                       [(h1_hi[:, g, cols], h1_lo[:, g, cols],
                                         ptT_hi[:, p2, 0, g], ptT_lo[:, p2, 0, g])])
                    if g == G - 1:
                        last.then_inc(ph_ready, 1)

            def conv1(s, k, g):
                if s.on(k):
                    pe.wait_ge(ph_done, s.n(k))
                    product(r_ps[g], times(ph, g, w1), B1).then_inc(r_ready[g], 1)

            def turn_r(s, k, g):
                if s.on(k):
                    pe.wait_ge(r_done[g], s.n(k))
                    blocks(rT_ps[g], r[:, g].rearrange("p (c n) -> p c n", n=N))\
                        .then_inc(rT_ready[g], 1)

            def conv2(s, k, g):
                if s.on(k):
                    pe.wait_ge(rT_done[g], s.n(k))
                    last = product(yp_ps[:, g], [(rT_hi[:, g, c], rT_lo[:, g, c],
                                                  w2_hi[:, c], w2_lo[:, c]) for c in range(KH)])
                    if g == G - 1:
                        last.then_inc(yp_ready, 1)

            def propagate2(s, k, g):
                if s.on(k):
                    pe.wait_ge(yp_done, s.n(k))
                    p2 = s.slot(k, 2)
                    last = product(conv_ps[:, g], [(ptT_hi[:, p2, 0, g], ptT_lo[:, p2, 0, g],
                                                    yp_hi[:, g], yp_lo[:, g])])
                    if g == G - 1:
                        last.then_inc(conv_ready, 1)

            def turn_h2(s, k):
                if s.on(k):
                    pe.wait_ge(normed_done[2], s.n(k))
                    blocks(h2T_ps, of_pair(normed[2])).then_inc(h2T_ready, 1)

            def qkv(s, k, g):
                if s.on(k):
                    pe.wait_ge(h2T_done, s.n(k))
                    last = product(qkv_ps[:, g], times(h2T, g, wqkv))
                    if g == G - 1:
                        last.then_inc(qkv_ready, 1)

            def mean_k(s, k, g):
                if s.on(k):
                    pe.wait_ge(k_done, s.n(k))
                    a4 = s.slot(k, UNROLL)
                    pe.matmul(ak_ps[:, g], aT_hi[:, a4, g], k_parts[:, g], start=True, stop=False)
                    last = pe.matmul(ak_ps[:, g, 0], aT_lo[:, a4, g], k_parts[:, g, 0],
                                     start=False, stop=True)
                    if g == G - 1:
                        last.then_inc(ak_ready, 1)

            def weight_rows(s, k):
                if s.on(k):
                    pe.wait_ge(w_done, s.n(k))
                    if s.past(k + 1):
                        pe.wait_ge(x4_relu_done, s.n(k + 1))
                    for g in range(G):
                        last = pe.transpose(wrow_ps[:, g], w[:, g:g + 1].broadcast_to([N, N]), ident[:])
                    last.then_inc(wrow_ready, 1)

            def turn_h3(s, k):
                if s.on(k):
                    pe.wait_ge(normed_done[3], s.n(k))
                    blocks(h3T_ps, of_pair(normed[3])).then_inc(h3T_ready, 1)

            def zb(s, k, g):
                if s.on(k):
                    pe.wait_ge(h3T_done, s.n(k))
                    last = product(zb_ps[:, g], times(h3T, g, w3, first=KD))
                    if g == G - 1:
                        last.then_inc(zb_ready, 1)

            def output(s, k, g):
                if s.on(k):
                    pe.wait_ge(zb_done, s.n(k))
                    a4 = s.slot(k, UNROLL)
                    last = product(out_ps[:, g], times(h3T, g, w3)
                                   + [(aT_hi[:, a4, g], aT_lo[:, a4, g], zb_hi[:, g], zb_lo[:, g])])
                    if g == G - 1:
                        last.then_inc(out_ready, 1)

            def step(s):
                qkv(s, 2, 1)
                output(s, 3, 1)
                y2(s, -1, 0)
                mean_k(s, 2, 0)
                y2(s, -1, 1)
                conv2(s, 1, 0)
                score_rows(s, -1)
                mean_k(s, 2, 1)
                conv2(s, 1, 1)
                weight_rows(s, 2)
                propagate(s, 0, 0)
                turn_adj(s, -2)
                propagate(s, 0, 1)
                gram(s, -1)
                propagate2(s, 1, 0)
                turn_h0(s, -2)
                propagate2(s, 1, 1)
                conv1(s, 0, 1)
                turn_pt(s, -1)
                conv1(s, 0, 0)
                y1(s, -1, 0)
                turn_r(s, 0, 1)
                turn_h3(s, 2)
                y1(s, -1, 1)
                turn_h2(s, 1)
                turn_r(s, 0, 0)
                zb(s, 2, 0)
                y0(s, -1, 0)
                zb(s, 2, 1)
                y0(s, -1, 1)
                qkv(s, 1, 0)
                output(s, 2, 0)

            steps(pe, step)

        @block.scalar
        def _(act):
            def copy(dst, src, func=ACT.Copy):
                return nc.scalar.activation(dst, src, func)

            def joined(t):
                return t[:].rearrange("p n j -> p (n j)")

            act.wait_ge(turned, 1)
            for dst, src in TURNED:
                copy(dst, src).then_inc(turned_sb, 1)
            act.wait_ge(bias_in, 16 * (BIAS_LOADS + 1))
            copy(bias_r[:], bias_f[:]).then_inc(hi_ready, 1)
            act.wait_ge(turned_sb, len(TURNED))
            act.wait_ge(u_ready, 1)
            act.wait_ge(w2_centred, 1)
            for src, hi, _ in SPLITS:
                copy(hi, src).then_inc(hi_ready, 1)

            def aT_part(s, k):
                if s.on(k):
                    act.wait_ge(aT_ready, s.n(k))
                    copy(aT_hi[:, s.slot(k, UNROLL)], aT_ps).then_inc(aT_hi_done, 1)

            def propagation(s, k):
                if s.on(k):
                    act.wait_ge(node_inv_done, s.n(k))
                    for g in range(G):
                        last = nc.scalar.activation(prop[:, s.slot(k, 2), g], gram_ps[:, g], ACT.Copy,
                                                    scale=node_inv[:, g])
                    last.then_inc(prop_done, 1)

            def ptT_part(s, k):
                if s.on(k):
                    act.wait_ge(ptT_ready, s.n(k))
                    copy(ptT_hi[:, s.slot(k, 2)].rearrange("p k g n -> p (k g n)"), ptT_ps)\
                        .then_inc(ptT_hi_done, 1)

            def h0T_part(s, k):
                if s.on(k):
                    act.wait_ge(h0T_ready, s.n(k))
                    if s.past(k + 1):
                        act.wait_ge(y0_ready, s.n(k + 1))
                    copy(joined(h0T_hi), h0T_ps, ACT.Relu).then_inc(h0T_hi_done, 1)

            def y2_part(s, k):
                if s.on(k):
                    act.wait_ge(y2_ready, s.n(k))
                    copy(y2_hi[:], y2_ps).then_inc(y2_hi_done, 1)

            def score_sum(s, k):
                if s.on(k):
                    act.wait_ge(e_ready, s.n(k))
                    for g in range(G):
                        last = nc.scalar.activation(z[:, g], e_ps[:, g], ACT.Identity,
                                                    bias=s_sb[:, g, 1:2])
                    last.then_inc(z_done, 1)

            def score_exp(s, k):
                if s.on(k):
                    act.wait_ge(leaky_done, s.n(k))
                    copy(z_exp[:], z_leaky[:], ACT.Exp).then_inc(exp_done, 1)

            def y1_part(s, k):
                if s.on(k):
                    act.wait_ge(y1_ready, s.n(k))
                    copy(y1_hi[:], y1_ps).then_inc(y1_hi_done, 1)

            def h1_relu(s, k):
                if s.on(k):
                    act.wait_ge(normed_done[1], s.n(k))
                    copy(h1[:], normed[1][:], ACT.Relu).then_inc(h1_done, 1)

            def h1_part(s, k):
                if s.on(k):
                    copy(h1_hi[:], normed[1][:], ACT.Relu).then_inc(h1_hi_done, 1)

            def ph_part(s, k):
                if s.on(k):
                    act.wait_ge(ph_ready, s.n(k))
                    copy(joined(ph_hi), ph_ps).then_inc(ph_hi_done, 1)

            def r_relu(s, k, g):
                if s.on(k):
                    act.wait_ge(r_ready[g], s.n(k))
                    nc.scalar.activation(r[:, g], r_ps[g], ACT.Relu, accum_out=r_sum[:, g:g + 1])\
                        .then_inc(r_done[g], 1)

            def r_squares(s, k, g):
                if s.on(k):
                    act.wait_ge(r_mean_done[g], s.n(k))
                    for n in range(KH):
                        chunk = slice(n * N, (n + 1) * N)
                        last = nc.scalar.activation(r_dev[:, chunk], r[:, g, chunk], ACT.Square,
                                                    bias=r_nmean[:, g:g + 1],
                                                    accum_out=r_part_ss[:, g, n:n + 1])
                    last.then_inc(r_squares_done[g], 1)

            def rT_part(s, k, g):
                if s.on(k):
                    act.wait_ge(rT_ready[g], s.n(k))
                    copy(rT_hi[:, g].rearrange("p c n -> p (c n)"), rT_ps[g])\
                        .then_inc(rT_hi_done[g], 1)

            def yp_part(s, k):
                if s.on(k):
                    act.wait_ge(yp_ready, s.n(k))
                    for g in range(G):
                        act.wait_ge(r_rstd_done[g], s.n(k))
                        last = nc.scalar.activation(yp_hi[:, g], yp_ps[:, g], ACT.Copy,
                                                    scale=r_rstd[:, g:g + 1])
                    last.then_inc(yp_hi_done, 1)

            def h2T_part(s, k):
                if s.on(k):
                    act.wait_ge(h2T_ready, s.n(k))
                    copy(joined(h2T_hi), h2T_ps, ACT.Relu).then_inc(h2T_hi_done, 1)

            def qkv_part(s, k):
                if s.on(k):
                    act.wait_ge(qkv_ready, s.n(k))
                    copy(k_parts[:, :, 0], qkv_ps[:, :, ATT:2 * ATT])
                    copy(q_sb[:], qkv_ps[:, :, :ATT])
                    copy(v_sb[:, s.slot(k, 2)], qkv_ps[:, :, 2 * ATT:]).then_inc(qkv_copied, 1)

            def weight_exp(s, k):
                if s.on(k):
                    act.wait_ge(w_nmax_done, s.n(k))
                    for g in range(G):
                        nc.scalar.activation(w_junk[:, g], wrow_ps[:, g], ACT.Exp,
                                             bias=w_nmax[:, g:g + 1], accum_out=w_sum[:, g:g + 1])
                    for g in range(G):
                        last = nc.scalar.activation(w_exp[:, g:g + 1], w[:, g:g + 1], ACT.Exp,
                                                    bias=w_nmax[:, g:g + 1])
                    last.then_inc(w_exp_done, 1)

            def h3T_part(s, k):
                if s.on(k):
                    act.wait_ge(h3T_ready, s.n(k))
                    copy(joined(h3T_hi), h3T_ps, ACT.Relu).then_inc(h3T_hi_done, 1)

            def zb_part(s, k):
                if s.on(k):
                    act.wait_ge(zb_ready, s.n(k))
                    for g in range(G):
                        last = nc.scalar.activation(zb_hi[:, g], zb_ps[:, g], ACT.Copy,
                                                    scale=deg_inv[:, s.slot(k, UNROLL), g:g + 1])
                    last.then_inc(zb_hi_done, 1)

            def out_relu(s, k):
                if s.on(k):
                    act.wait_ge(out_ready, s.n(k))
                    for g in range(G):
                        last = nc.scalar.activation(x4_relu[:, g], out_ps[:, g], ACT.Relu,
                                                    scale=deg_inv[:, s.slot(k, UNROLL), g:g + 1])
                    last.then_inc(x4_relu_done, 1)

            def step(s):
                qkv_part(s, 2)
                out_relu(s, 3)
                aT_part(s, -1)
                h1_relu(s, 0)
                y2_part(s, -1)
                h1_part(s, 0)
                score_sum(s, -1)
                score_exp(s, -1)
                yp_part(s, 1)
                weight_exp(s, 2)
                ph_part(s, 0)
                propagation(s, -1)
                ptT_part(s, -1)
                r_relu(s, 0, 1)
                r_relu(s, 0, 0)
                r_squares(s, 0, 1)
                rT_part(s, 0, 1)
                h3T_part(s, 2)
                y1_part(s, -1)
                rT_part(s, 0, 0)
                h2T_part(s, 1)
                zb_part(s, 2)
                h0T_part(s, -2)
                r_squares(s, 0, 0)

            steps(act, step)

        @block.vector
        def _(dve):
            def rest(dst, src, hi):
                return dve.tensor_tensor(dst, src, hi.bitcast(F32), ALU.subtract)

            def scaled_rest(dst, src, scale, hi):
                return dve.scalar_tensor_tensor(out=dst, in0=src, scalar=scale, in1=hi.bitcast(F32),
                                                op0=ALU.mult, op1=ALU.subtract)

            def relu_rest(dst, src, hi):
                return dve.scalar_tensor_tensor(out=dst, in0=src, scalar=0.0, in1=hi.bitcast(F32),
                                                op0=ALU.max, op1=ALU.subtract)

            def joined(t):
                return t[:].rearrange("p n j -> p (n j)")

            dve.wait_ge(loaded, 16 * LOADS)
            n = 0
            for c in range(KD):
                for h in range(2):
                    n += 1
                    dve.scalar_tensor_tensor(out=junk[:], in0=n_wv0[:, c], scalar=1.0,
                                             in1=aw_rows[:, h], op0=ALU.mult, op1=ALU.mult,
                                             accum_out=wk_f[:, c, HOPS * D + h:HOPS * D + h + 1])\
                       .then_inc(kappa_ready, 1)
                    dve.wait_ge(kappa_ready, n)
            for h in range(2):
                n += 1
                dve.scalar_tensor_tensor(out=junk[:], in0=bv_rows[:], scalar=1.0, in1=aw_rows[:, h],
                                         op0=ALU.mult, op1=ALU.mult, accum_out=kappa[:, h:h + 1])\
                   .then_inc(kappa_ready, 1)
                dve.wait_ge(kappa_ready, n)
            dve.tensor_tensor(kappa1[:], kappa[:, 0:1], kappa[:, 1:2], ALU.add)\
               .then_inc(kappa_ready, 1)
            dve.wait_ge(kappa_ready, n + 1)
            dve.tensor_scalar(s_const[:], kappa1[:], ab_rows[:, 0:1], 0.5, ALU.add, ALU.mult)\
               .then_inc(u_ready, 1)
            dve.wait_ge(turned_sb, 4)
            for c in range(KH):
                last = dve.tensor_scalar(t_w2g[:, c], t_w2[c], gamma_t[:, c:c + 1], None,
                                         ALU.mult)
            last.then_inc(w2_scaled, 1)
            dve.wait_ge(w2_mean_ready, 1)
            dve.tensor_tensor(t_w2g[:], t_w2g[:], psum[:, 1, 0:D].unsqueeze(1).broadcast_to([N, KH, D]),
                              ALU.subtract).then_inc(w2_centred, 1)
            dve.wait_ge(hi_ready, 1)
            rest(bias_r[32:64, :], bias_f[32:64, :], bias_r[32:64, :])
            dve.wait_ge(bw_ready, 1)
            dve.tensor_copy(bw_all[:], psum[:, 0, 0:D])
            dve.wait_ge(u_ready, 1)
            dve.wait_ge(w2_centred, 1)
            for n, (src, hi, lo) in enumerate(SPLITS):
                dve.wait_ge(hi_ready, n + 2)
                last = rest(lo, src, hi)
            last.then_inc(weights_ready, 1)

            def norm_stats(layer, src, count):
                for g in range(G):
                    last = dve.bn_stats(stats[layer][:, g], src[:, g])
                last.then_inc(stats_done[layer], 1)
                dve.wait_ge(stats_done[layer], count)
                dve.memset(held[:], 0.0)
                for g in range(G):
                    last = dve.bn_aggr(moments[layer][:, g], stats[layer][:, g])
                last.then_inc(moments_done[layer], 1)

            def norm(layer, src, scale):
                for g in range(G):
                    last = dve.tensor_scalar(normed[layer][:, g], src[:, g],
                                             moments[layer][:, g, 0:1], scale[:, g:g + 1],
                                             ALU.subtract, ALU.mult)
                last.then_inc(normed_done[layer], 1)

            def stats0(s, k):
                if s.on(k):
                    x4_slot = s.slot(k, UNROLL)
                    dve.wait_ge(pair_loaded[x4_slot], s.loads(k))
                    norm_stats(0, x_in[:, x4_slot], s.n(k))

            def norm0(s, k):
                if s.on(k):
                    if s.past(k + 1):
                        dve.wait_ge(h0T_ready, s.n(k + 1))
                    dve.wait_ge(rstd_done[0], s.n(k))
                    norm(0, x_in[:, s.slot(k, UNROLL)], rstd[0])

            def degrees(s, k):
                if s.on(k):
                    a4 = s.slot(k, UNROLL)
                    dve.wait_ge(pair_loaded[a4], s.loads(k))
                    dve.tensor_reduce(deg[:], a_in[:, a4], AX_X, ALU.add).then_inc(deg_done, 1)
                    dve.wait_ge(deg_done, s.n(k))
                    dve.tensor_scalar(deg_max[:, a4], deg[:], DEG_EPS, None, ALU.max)\
                       .then_inc(deg_max_done, 1)
                    dve.wait_ge(deg_max_done, s.n(k))
                    dve.reciprocal(deg_inv[:, a4], deg_max[:, a4]).then_inc(deg_inv_done, 1)

            def incidence(s, k):
                if s.on(k):
                    a4 = s.slot(k, UNROLL)
                    edge_col = (slice(None), slice(None), slice(N, N + 1))
                    dve.wait_ge(aT_hi_done, s.n(k))
                    dve.tensor_scalar(inc_t[:], aT_ps, 0.0, None, ALU.not_equal)\
                       .then_inc(inc_done, 1)
                    dve.tensor_copy(binc_hi[edge_col], aT_ps[:, :, 0:1])
                    rest(aT_lo[:, a4], aT_ps, aT_hi[:, a4]).then_inc(aT_done, 1)
                    dve.wait_ge(inc_done, s.n(k))
                    dve.tensor_reduce(edge_cnt[:], inc_t[:].bitcast(F32), AX_X, ALU.add)\
                       .then_inc(edge_cnt_done, 1)
                    dve.wait_ge(aT_done, s.n(k))
                    rest(binc_lo[edge_col], aT_ps[:, :, 0:1], binc_hi[edge_col])\
                        .then_inc(edge_w_done, 1)

            def edge_sizes(s, k):
                if s.on(k):
                    dve.wait_ge(edge_cnt_done, s.n(k))
                    dve.tensor_scalar(edge_cnt1[:], edge_cnt[:], 1.0, None, ALU.max)\
                       .then_inc(edge_cnt1_done, 1)
                    dve.wait_ge(edge_cnt1_done, s.n(k))
                    dve.reciprocal(edge_inv[:], edge_cnt1[:]).then_inc(edge_inv_done, 1)
                    dve.wait_ge(edge_inv_done, s.n(k))
                    dve.tensor_copy(einv_hi[:], edge_inv[:]).then_inc(einv_hi_done, 1)
                    dve.wait_ge(einv_hi_done, s.n(k))
                    rest(einv_lo[:], edge_inv[:], einv_hi[:]).then_inc(einv_done, 1)

            def node_sizes(s, k):
                if s.on(k):
                    dve.wait_ge(gram_ready, s.n(k))
                    dve.tensor_scalar(node_w1[:], gram_ps[:, :, N:N + 1], TINY, None, ALU.max)\
                       .then_inc(node_w1_done, 1)
                    dve.wait_ge(node_w1_done, s.n(k))
                    dve.reciprocal(node_w2[:], node_w1[:]).then_inc(node_w2_done, 1)
                    dve.wait_ge(node_w2_done, s.n(k))
                    dve.scalar_tensor_tensor(out=node_inv[:], in0=gram_ps[:, :, N:N + 1], scalar=0.0,
                                             in1=node_w2[:], op0=ALU.is_gt, op1=ALU.mult)\
                       .then_inc(node_inv_done, 1)

            def ptT_rest(s, k):
                if s.on(k):
                    t2 = s.slot(k, 2)
                    dve.wait_ge(ptT_hi_done, s.n(k))
                    rest(ptT_lo[:, t2].rearrange("p k g n -> p (k g n)"), ptT_ps,
                         ptT_hi[:, t2].rearrange("p k g n -> p (k g n)")).then_inc(ptT_done, 1)

            def h0T_rest(s, k):
                if s.on(k):
                    dve.wait_ge(h0T_hi_done, s.n(k))
                    relu_rest(joined(h0T_lo), h0T_ps, joined(h0T_hi)).then_inc(h0T_done, 1)

            def scores(s, k):
                if s.on(k):
                    dve.wait_ge(y2_hi_done, s.n(k))
                    dve.tensor_scalar(s_sb[:], s_ps, s_const[:, 0:1], None, ALU.add)\
                       .then_inc(s_done, 1)

            def y2_rest(s, k):
                if s.on(k):
                    rest(y2_lo[:], y2_ps, y2_hi[:]).then_inc(y2_done, 1)

            def leaky(s, k):
                if s.on(k):
                    dve.wait_ge(z_done, s.n(k))
                    dve.scalar_tensor_tensor(out=z_leaky[:], in0=z[:], scalar=SLOPE, in1=z[:],
                                             op0=ALU.mult, op1=ALU.max).then_inc(leaky_done, 1)

            def alphas(s, k):
                if s.on(k):
                    dve.wait_ge(exp_done, s.n(k))
                    for g in range(G):
                        last = dve.scalar_tensor_tensor(out=alpha[:, g], in0=z_exp[:, g], scalar=1.0,
                                                        in1=a_in[:, s.slot(k, UNROLL), g],
                                                        op0=ALU.mult, op1=ALU.mult,
                                                        accum_out=row_sum[:, g:g + 1])
                    last.then_inc(alpha_done, 1)

            def row_sums(s, k):
                if s.on(k):
                    dve.wait_ge(alpha_done, s.n(k))
                    dve.tensor_scalar(row_sum1[:], row_sum[:], ROW_EPS, None, ALU.add)\
                       .then_inc(row_sum_done, 1)
                    dve.wait_ge(row_sum_done, s.n(k))
                    dve.reciprocal(row_inv[:], row_sum1[:]).then_inc(row_inv_done, 1)

            def y1_rest(s, k):
                if s.on(k):
                    dve.wait_ge(y1_hi_done, s.n(k))
                    rest(y1_lo[:], y1_ps, y1_hi[:]).then_inc(y1_done, 1)

            def sum1(s, k):
                if s.on(k):
                    dve.wait_ge(y0_ready, s.n(k))
                    if s.past(k + 1):
                        dve.wait_ge(x1b_done, s.n(k + 1))
                    dve.scalar_tensor_tensor(out=x1[:], in0=y0_ps, scalar=0.0,
                                             in1=x_in[:, s.slot(k, UNROLL)],
                                             op0=ALU.max, op1=ALU.add).then_inc(x1_done, 1)

            def stats1(s, k):
                if s.on(k):
                    dve.wait_ge(x1_done, s.n(k))
                    norm_stats(1, x1, s.n(k))

            def norm1(s, k):
                if s.on(k):
                    dve.wait_ge(rstd_done[1], s.n(k))
                    norm(1, x1, rstd[1])

            def ph_rest(s, k):
                if s.on(k):
                    dve.wait_ge(ph_hi_done, s.n(k))
                    rest(joined(ph_lo), ph_ps, joined(ph_hi)).then_inc(ph_done, 1)

            def rT_rest(s, k, g):
                if s.on(k):
                    dve.wait_ge(rT_hi_done[g], s.n(k))
                    rest(rT_lo[:, g].rearrange("p c n -> p (c n)"), rT_ps[g],
                         rT_hi[:, g].rearrange("p c n -> p (c n)")).then_inc(rT_done[g], 1)

            def yp_rest(s, k):
                if s.on(k):
                    dve.wait_ge(yp_hi_done, s.n(k))
                    for g in range(G):
                        last = scaled_rest(yp_lo[:, g], yp_ps[:, g], r_rstd[:, g:g + 1], yp_hi[:, g])
                    last.then_inc(yp_done, 1)

            def sum2(s, k):
                if s.on(k):
                    dve.wait_ge(conv_ready, s.n(k))
                    dve.wait_ge(xh_done, s.n(k))
                    dve.tensor_tensor(x2[:, s.slot(k, 2)], conv_ps, xh[:, s.slot(k, 2)], ALU.add)\
                       .then_inc(x2_done, 1)

            def stats2(s, k):
                if s.on(k):
                    dve.wait_ge(x2_done, s.n(k))
                    norm_stats(2, x2[:, s.slot(k, 2)], s.n(k))

            def norm2(s, k):
                if s.on(k):
                    dve.wait_ge(rstd_done[2], s.n(k))
                    norm(2, x2[:, s.slot(k, 2)], rstd[2])

            def h2T_rest(s, k):
                if s.on(k):
                    dve.wait_ge(h2T_hi_done, s.n(k))
                    relu_rest(joined(h2T_lo), h2T_ps, joined(h2T_hi)).then_inc(h2T_done, 1)

            def k_rest(s, k):
                if s.on(k):
                    dve.wait_ge(qkv_copied, s.n(k))
                    rest(k_parts[:, :, 1], qkv_ps[:, :, ATT:2 * ATT], k_parts[:, :, 0])\
                       .then_inc(k_done, 1)

            def weights(s, k):
                if s.on(k):
                    dve.wait_ge(ak_ready, s.n(k))
                    for g in range(G):
                        q_twice = q_sb[:, g:g + 1].broadcast_to([N, 2, ATT])
                        last = dve.scalar_tensor_tensor(out=qk_junk[:, g], in0=ak_ps[:, g],
                                                        scalar=float(ATT) ** -0.5, in1=q_twice,
                                                        op0=ALU.mult, op1=ALU.mult,
                                                        accum_out=w[:, g:g + 1])
                    last.then_inc(w_done, 1)

            def weight_max(s, k):
                if s.on(k):
                    dve.wait_ge(wrow_ready, s.n(k))
                    dve.tensor_reduce(w_nmax[:], wrow_ps, AX_X, ALU.max, negate=True)\
                       .then_inc(w_nmax_done, 1)

            def softmax(s, k):
                if s.on(k):
                    dve.wait_ge(w_exp_done, s.n(k))
                    dve.reciprocal(w_inv[:], w_sum[:]).then_inc(w_inv_done, 1)
                    dve.wait_ge(w_inv_done, s.n(k))
                    dve.tensor_tensor(w_soft[:], w_exp[:], w_inv[:], ALU.mult)\
                       .then_inc(w_soft_done, 1)

            def sum3(s, k):
                if s.on(k):
                    dve.wait_ge(w_soft_done, s.n(k))
                    for g in range(G):
                        last = dve.scalar_tensor_tensor(out=x3[:, s.slot(k, 2), g],
                                                        in0=v_sb[:, s.slot(k, 2), g],
                                                        scalar=w_soft[:, g:g + 1],
                                                        in1=x2[:, s.slot(k, 2), g],
                                                        op0=ALU.mult, op1=ALU.add)
                    last.then_inc(x3_done, 1)

            def stats3(s, k):
                if s.on(k):
                    dve.wait_ge(x3_done, s.n(k))
                    norm_stats(3, x3[:, s.slot(k, 2)], s.n(k))

            def norm3(s, k):
                if s.on(k):
                    dve.wait_ge(rstd_deg_done, s.n(k))
                    norm(3, x3[:, s.slot(k, 2)], rstd_deg)

            def h3T_rest(s, k):
                if s.on(k):
                    dve.wait_ge(h3T_hi_done, s.n(k))
                    relu_rest(joined(h3T_lo), h3T_ps, joined(h3T_hi)).then_inc(h3T_done, 1)

            def zb_rest(s, k):
                if s.on(k):
                    dve.wait_ge(zb_hi_done, s.n(k))
                    for g in range(G):
                        last = scaled_rest(zb_lo[:, g], zb_ps[:, g],
                                           deg_inv[:, s.slot(k, UNROLL), g:g + 1], zb_hi[:, g])
                    last.then_inc(zb_done, 1)

            def step(s):
                stats1(s, 0)
                h0T_rest(s, -1)
                norm0(s, -2)
                norm1(s, 0)
                k_rest(s, 2)
                stats0(s, -3)
                incidence(s, -1)
                scores(s, -1)
                edge_sizes(s, -1)
                weights(s, 2)
                leaky(s, -1)
                y2_rest(s, -1)
                weight_max(s, 2)
                alphas(s, -1)
                yp_rest(s, 1)
                softmax(s, 2)
                row_sums(s, -1)
                ph_rest(s, 0)
                node_sizes(s, -1)
                sum3(s, 2)
                sum2(s, 1)
                stats3(s, 2)
                ptT_rest(s, -1)
                stats2(s, 1)
                norm3(s, 2)
                degrees(s, -1)
                norm2(s, 1)
                h3T_rest(s, 2)
                y1_rest(s, -1)
                rT_rest(s, 0, 1)
                h2T_rest(s, 1)
                rT_rest(s, 0, 0)
                zb_rest(s, 2)
                sum1(s, -1)

            steps(dve, step)

        @block.gpsimd
        def _(pool):
            pool.memset(bias_f[:], 0.0).then_inc(zeroed, 1)
            pool.memset(binc_hi[:].bitcast(F32), 0.0).then_inc(zeroed, 1)
            pool.memset(binc_lo[:].bitcast(F32), 0.0).then_inc(zeroed, 1)
            pool.memset(hid_inv[:], 1.0 / HID).then_inc(consts, 1)
            pool.memset(hid_ninv[:], -1.0 / HID).then_inc(consts, 1)
            pool.memset(ones_r[:].bitcast(F32), 1.0).then_inc(consts, 1)
            pool.memset(eps_ln[:], LN_EPS).then_inc(consts, 1)
            pool.memset(minus_half[:], -0.5).then_inc(consts, 1)
            pool.memset(ident[:], 0.0).then_inc(consts, 1)
            pool.wait_ge(consts, 6)
            pool.affine_select(out=ident[:], in_=ident[:], compare_op=ALU.not_equal, fill=1.0, base=0,
                               pattern=[[-1, N]], channel_multiplier=1).then_inc(consts, 2)
            pool.wait_ge(consts, 8)
            pool.wait_ge(zeroed, 3)
            pool.memset(binc_hi[:, :, N + 1:N + 2].bitcast(F32), 1.0)
            pool.wait_ge(bias_in, 16 * (BIAS_LOADS + 1))

            def inverse_std(s, k, layer):
                if s.on(k):
                    pool.wait_ge(moments_done[layer], s.n(k))
                    pool.tensor_tensor(var_eps[layer][:], moments[layer][:, :, 1], eps_ln[:], ALU.add)\
                        .then_inc(var_done[layer], 1)
                    pool.wait_ge(var_done[layer], s.n(k))
                    pool.tensor_tensor(rstd[layer][:], var_eps[layer][:], minus_half[:], ALU.pow)\
                        .then_inc(rstd_done[layer], 1)

            def times_degree(s, k):
                if s.on(k):
                    pool.wait_ge(rstd_done[3], s.n(k))
                    pool.wait_ge(deg_inv_done, s.n(k))
                    pool.tensor_tensor(rstd_deg[:], rstd[3][:], deg_max[:, s.slot(k, UNROLL)], ALU.mult)\
                        .then_inc(rstd_deg_done, 1)

            def r_mean(s, k, g):
                if s.on(k):
                    pool.wait_ge(r_done[g], s.n(k))
                    pool.tensor_tensor(r_nmean[:, g:g + 1], r_sum[:, g:g + 1], hid_ninv[:, g:g + 1],
                                       ALU.mult).then_inc(r_mean_done[g], 1)

            def r_inverse_std(s, k, g):
                if s.on(k):
                    one = slice(g, g + 1)
                    pool.wait_ge(r_squares_done[g], s.n(k))
                    pool.tensor_tensor(r_half_ss[:, g], r_part_ss[:, g, 0:2], r_part_ss[:, g, 2:4],
                                       ALU.add).then_inc(r_half_ss_done[g], 1)
                    pool.wait_ge(r_half_ss_done[g], s.n(k))
                    pool.tensor_tensor(r_ss[:, one], r_half_ss[:, g, 0:1], r_half_ss[:, g, 1:2],
                                       ALU.add).then_inc(r_ss_done[g], 1)
                    pool.wait_ge(r_ss_done[g], s.n(k))
                    pool.tensor_tensor(r_var[:, one], r_ss[:, one], hid_inv[:, one], ALU.mult)\
                        .then_inc(r_var_done[g], 1)
                    pool.wait_ge(r_var_done[g], s.n(k))
                    pool.tensor_tensor(r_var_eps[:, one], r_var[:, one], eps_ln[:, one], ALU.add)\
                        .then_inc(r_var_eps_done[g], 1)
                    pool.wait_ge(r_var_eps_done[g], s.n(k))
                    pool.tensor_tensor(r_rstd[:, one], r_var_eps[:, one], minus_half[:, one],
                                       ALU.pow).then_inc(r_rstd_done[g], 1)

            def rows(v):
                return v.unsqueeze(2).broadcast_to([N, G, N])

            def scaled_incidence(s, k):
                if s.on(k):
                    pool.wait_ge(einv_done, s.n(k))
                    pool.tensor_tensor(binc_hi[:, :, 0:N], inc_t[:].bitcast(F32),
                                       rows(einv_hi[:].bitcast(F32)), ALU.mult)
                    pool.tensor_tensor(binc_lo[:, :, 0:N], inc_t[:].bitcast(F32),
                                       rows(einv_lo[:].bitcast(F32)), ALU.mult)\
                        .then_inc(binc_done, 1)

            def transition(s, k):
                if s.on(k):
                    pool.wait_ge(row_inv_done, s.n(k))
                    pool.tensor_tensor(trans[:], alpha[:], rows(row_inv[:]), ALU.mult)\
                        .then_inc(trans_done, 1)

            def h1_rest(s, k):
                if s.on(k):
                    pool.wait_ge(h1_hi_done, s.n(k))
                    pool.tensor_tensor(h1_lo[:], h1[:], h1_hi[:].bitcast(F32), ALU.subtract)\
                        .then_inc(h1_lo_done, 1)

            def residual1(s, k):
                if s.on(k):
                    pool.wait_ge(h1_done, s.n(k))
                    pool.tensor_tensor(x1b[:], x1[:], b2_rows[:].unsqueeze(1).broadcast_to([N, G, D]),
                                       ALU.add).then_inc(x1b_done, 1)
                    pool.tensor_tensor(p_bw[:], prop[:, s.slot(k, 2), :, N + 1:N + 2].broadcast_to([N, G, D]),
                                       bw_all[:].unsqueeze(1).broadcast_to([N, G, D]), ALU.mult)
                    pool.wait_ge(x1b_done, s.n(k))
                    pool.tensor_tensor(xbh[:], x1b[:], h1[:], ALU.add).then_inc(xbh_done, 1)
                    pool.wait_ge(xbh_done, s.n(k))
                    pool.tensor_tensor(xh[:, s.slot(k, 2)], xbh[:], p_bw[:], ALU.add)\
                        .then_inc(xh_done, 1)

            def sum4(s, k):
                if s.on(k):
                    pool.wait_ge(x4_relu_done, s.n(k))
                    if s.past(k + 1):
                        pool.wait_ge(stored, 16 * s.n(k + 1))
                    pool.tensor_tensor(x4[:], x4_relu[:], x3[:, s.slot(k, 2)], ALU.add)\
                        .then_inc(x4_done, 1)

            def step(s):
                inverse_std(s, 0, 1)
                r_inverse_std(s, 1, 1)
                sum4(s, 3)
                r_inverse_std(s, 1, 0)
                h1_rest(s, 0)
                scaled_incidence(s, -1)
                transition(s, -1)
                inverse_std(s, 2, 3)
                times_degree(s, 2)
                r_mean(s, 0, 1)
                inverse_std(s, 1, 2)
                residual1(s, 0)
                r_mean(s, 0, 0)
                inverse_std(s, -3, 0)

            steps(pool, step)


_INS = ['x', 'adj', 'L0_gnn_Wv', 'L0_gnn_bv', 'L0_gnn_aw', 'L0_gnn_ab', 'L0_gnn_Wk', 'L0_gnn_bk',
        'L1_gnn_W1', 'L1_gnn_b1', 'L1_gnn_gamma', 'L1_gnn_beta', 'L1_gnn_W2', 'L1_gnn_b2',
        'L2_gnn_W_qk', 'L2_gnn_W_v', 'L3_gnn_W']


def kernel(**inputs):
    import numpy as np
    import concourse.bacc as bacc
    from concourse.bass_utils import run_bass_kernel_spmd

    nc = bacc.Bacc("TRN2", target_bir_lowering=False, num_devices=1)
    arrays, args = {}, []
    for name in _INS:
        a = np.ascontiguousarray(inputs[name])
        arrays[f"in_{name}"] = a
        args.append(nc.dram_tensor(f"in_{name}", a.shape, mybir.dt.from_np(a.dtype),
                                   kind="ExternalInput").ap())
    out = nc.dram_tensor("out_x", inputs["x"].shape, F32, kind="ExternalOutput").ap()
    build_program(nc, *args, out)
    result = run_bass_kernel_spmd(nc, [arrays], core_ids=[0])
    return result.results[0]["out_x"]
```
